# Optimizing a Trainium2 kernel written in Bass

```python
import numpy as np
import jax
import jax.numpy as jnp

def _softmax(x, axis=-1):
    return jax.nn.softmax(x, axis=axis)

def _gelu(x):
    return jax.nn.gelu(x, approximate=True)

def _silu(x):
    return jax.nn.silu(x)

def _sigmoid(x):
    return jax.nn.sigmoid(x)

def _layernorm(x, axis=-1, eps=1e-05):
    m = jnp.mean(x, axis=axis, keepdims=True)
    v = jnp.var(x, axis=axis, keepdims=True)
    return (x - m) / jnp.sqrt(v + eps)

def _scatter_add(tgt, idx, src, axis=0):
    return tgt.at[idx].add(src)

def _segment_sum(src, seg, n):
    return jax.ops.segment_sum(src, seg, n)
kernel_name = 'mk_flamingo_gated_d1_seqx_r8_9343a5'

def setup_inputs(seed: int=0):
    np.random.seed(seed)
    _w = jnp.asarray

    def _rec_inputs():
        import jax
        import jax.numpy as jnp
        _rk = jax.random.key(seed)
        x = 7.22e-05 + 1 * jax.random.normal(jax.random.fold_in(_rk, 1), (8, 128, 512), jnp.float32)
        _lenS = 128 - jax.random.randint(jax.random.fold_in(_rk, 7), (8,), 0, max(1, 128 // 4) + 1, jnp.int32)
        _lenS2 = 128 - jax.random.randint(jax.random.fold_in(_rk, 8), (8,), 0, max(1, 128 // 4) + 1, jnp.int32)
        _ctx_4096P = jax.random.normal(jax.random.fold_in(_rk, 11), (8, 16, 512), jnp.float32)
        _ctx_4096c = jax.random.dirichlet(jax.random.fold_in(_rk, 511), 0.3 * jnp.ones((16,), jnp.float32), (8, 128))
        _ctx_4096t = jnp.einsum('bsk,bkd->bsd', _ctx_4096c, _ctx_4096P)
        _ctx_4096t = _ctx_4096t * jax.lax.rsqrt(jnp.mean(jnp.square(_ctx_4096t)) + 1e-12) * 0.953939
        ctx_4096 = 4.13588e-05 + 0.999923 * (_ctx_4096t + 0.3 * jax.random.normal(jax.random.fold_in(_rk, 611), (8, 128, 512), jnp.float32))
        _validS = jnp.arange(128)[None, :] < _lenS[:, None]
        _validS2 = jnp.arange(128)[None, :] < _lenS2[:, None]
        _causal = jnp.tril(jnp.ones((128, 128), dtype=bool))
        mask_BxSxS2_ff1 = jnp.where(jnp.ones((8, 128, 128), dtype=bool), 1.0, 0.0).astype(jnp.float32)
        _g = jax.random.normal(jax.random.fold_in(_rk, 9001), (2, 1), jnp.float32)
        _g = jnp.sign(_g) * jnp.maximum(jnp.abs(_g), 1.0) + (_g == 0) * 1.0
        g_xattn = _g[0]
        g_ffn = _g[1]
        return (x, ctx_4096, mask_BxSxS2_ff1, g_xattn, g_ffn)
    x, ctx_4096, mask_BxSxS2_ff1, g_xattn, g_ffn = _rec_inputs()

    def _L0_xattn_setup():
        import jax, jax.numpy as jnp
        import numpy as np
        N_Q_HEADS = 32
        N_KV_HEADS = 8
        D_MODEL = 512
        D_K = 128
        D_V = 128
        ROPE_BASE = 10000.0

        def _rope(x):
            d = x.shape[-1]
            s = x.shape[2]
            inv_freq = 1.0 / ROPE_BASE ** (jnp.arange(0, d, 2, dtype=jnp.float32) / d)
            ang = jnp.arange(s, dtype=jnp.float32)[:, None] * inv_freq[None, :]
            cos = jnp.concatenate([jnp.cos(ang), jnp.cos(ang)], axis=-1)[None, None]
            sin = jnp.concatenate([jnp.sin(ang), jnp.sin(ang)], axis=-1)[None, None]
            x1, x2 = (x[..., :d // 2], x[..., d // 2:])
            rot = jnp.concatenate([-x2, x1], axis=-1)
            return x * cos + rot * sin
        key = jax.random.key(seed)
        ks = jax.random.split(key, 8)
        bs, s = (2, 128)
        inp = {'query': jax.random.normal(ks[0], (bs, s, D_MODEL), dtype=jnp.float32), 'key': jax.random.normal(ks[1], (bs, s, D_MODEL), dtype=jnp.float32), 'value': jax.random.normal(ks[2], (bs, s, D_MODEL), dtype=jnp.float32), 'mask': jnp.ones((bs, s, s), dtype=jnp.float32), 'wq': jax.random.normal(ks[3], (D_MODEL, N_Q_HEADS * D_K), dtype=jnp.float32) * 0.02, 'wk': jax.random.normal(ks[4], (D_MODEL, N_KV_HEADS * D_K), dtype=jnp.float32) * 0.02, 'wv': jax.random.normal(ks[5], (D_MODEL, N_KV_HEADS * D_V), dtype=jnp.float32) * 0.02, 'wo': jax.random.normal(ks[6], (N_Q_HEADS * D_V, D_MODEL), dtype=jnp.float32) * 0.02}
        return inp
    _L0_xattn_all = _L0_xattn_setup()
    _L0_xattn_in = {k: v for k, v in _L0_xattn_all.items() if k in ('wq', 'wk', 'wv', 'wo')}
    del _L0_xattn_all

    def _L0_ffn_setup():
        import jax, jax.numpy as jnp
        import numpy as np
        D_MODEL = 512
        D_FF = 1376
        key = jax.random.key(seed)
        k1, k2, k3, k4 = jax.random.split(key, 4)
        x = jax.random.normal(k1, (2, 256, D_MODEL), dtype=jnp.float32)
        W_gate = jax.random.normal(k2, (D_FF, D_MODEL), dtype=jnp.float32) * D_MODEL ** (-0.5)
        W_up = jax.random.normal(k3, (D_FF, D_MODEL), dtype=jnp.float32) * D_MODEL ** (-0.5)
        W_down = jax.random.normal(k4, (D_MODEL, D_FF), dtype=jnp.float32) * D_FF ** (-0.5)
        return {'x': x, 'W_gate': W_gate, 'W_up': W_up, 'W_down': W_down}
    _L0_ffn_all = _L0_ffn_setup()
    _L0_ffn_in = {k: v for k, v in _L0_ffn_all.items() if k in ('W_gate', 'W_up', 'W_down')}
    del _L0_ffn_all
    return {'x': x, 'ctx_4096': ctx_4096, 'mask_BxSxS2_ff1': mask_BxSxS2_ff1, 'g_xattn': g_xattn, 'g_ffn': g_ffn, 'L0_xattn_wq': _L0_xattn_in['wq'], 'L0_xattn_wk': _L0_xattn_in['wk'], 'L0_xattn_wv': _L0_xattn_in['wv'], 'L0_xattn_wo': _L0_xattn_in['wo'], 'L0_ffn_W_gate': _L0_ffn_in['W_gate'], 'L0_ffn_W_up': _L0_ffn_in['W_up'], 'L0_ffn_W_down': _L0_ffn_in['W_down']}

def reference(x, ctx_4096, mask_BxSxS2_ff1, g_xattn, g_ffn, L0_xattn_wq, L0_xattn_wk, L0_xattn_wv, L0_xattn_wo, L0_ffn_W_gate, L0_ffn_W_up, L0_ffn_W_down):
    import jax
    import jax.numpy as jnp

    def _L0_xattn_ref(query, key, value, mask, wq, wk, wv, wo):
        import jax, jax.numpy as jnp
        import numpy as np
        N_Q_HEADS = 32
        N_KV_HEADS = 8
        D_MODEL = 512
        D_K = 128
        D_V = 128
        ROPE_BASE = 10000.0

        def _rope(x):
            d = x.shape[-1]
            s = x.shape[2]
            inv_freq = 1.0 / ROPE_BASE ** (jnp.arange(0, d, 2, dtype=jnp.float32) / d)
            ang = jnp.arange(s, dtype=jnp.float32)[:, None] * inv_freq[None, :]
            cos = jnp.concatenate([jnp.cos(ang), jnp.cos(ang)], axis=-1)[None, None]
            sin = jnp.concatenate([jnp.sin(ang), jnp.sin(ang)], axis=-1)[None, None]
            x1, x2 = (x[..., :d // 2], x[..., d // 2:])
            rot = jnp.concatenate([-x2, x1], axis=-1)
            return x * cos + rot * sin
        bs, s, _ = query.shape
        g = N_Q_HEADS // N_KV_HEADS
        q = (query @ wq).reshape(bs, s, N_Q_HEADS, D_K).transpose(0, 2, 1, 3)
        k = (key @ wk).reshape(bs, s, N_KV_HEADS, D_K).transpose(0, 2, 1, 3)
        v = (value @ wv).reshape(bs, s, N_KV_HEADS, D_V).transpose(0, 2, 1, 3)
        q = _rope(q)
        k = _rope(k)
        scale = jnp.sqrt(jnp.float32(D_K))
        qg = q.reshape(bs, N_KV_HEADS, g, s, D_K)
        scores = jnp.einsum('bhgqd,bhkd->bhgqk', qg, k) / scale
        masked = jnp.where(mask[:, None, None].astype(bool), scores, -1000000000.0)
        w = jax.nn.softmax(masked, axis=-1)
        out = jnp.einsum('bhgqk,bhkd->bhgqd', w, v)
        out = out.reshape(bs, N_Q_HEADS, s, D_V).transpose(0, 2, 1, 3).reshape(bs, s, N_Q_HEADS * D_V)
        return out @ wo

    def _L0_ffn_ref(x, W_gate, W_up, W_down):
        import jax, jax.numpy as jnp
        import numpy as np
        D_MODEL = 512
        D_FF = 1376
        out_shape = x.shape[:-1] + (W_down.shape[0],)
        xf = x.reshape(-1, x.shape[-1])
        up = jnp.einsum('td,fd->tf', xf, W_up)
        gate = jax.nn.silu(jnp.einsum('td,fd->tf', xf, W_gate))
        h = gate * up
        y = jnp.einsum('tf,df->td', h, W_down)
        return y.reshape(out_shape)
    x = x + jnp.tanh(g_xattn[0]) * _L0_xattn_ref(_layernorm(x, axis=-1), ctx_4096, ctx_4096, mask_BxSxS2_ff1, L0_xattn_wq, L0_xattn_wk, L0_xattn_wv, L0_xattn_wo)
    x = x + jnp.tanh(g_ffn[0]) * _L0_ffn_ref(_layernorm(x, axis=-1), L0_ffn_W_gate, L0_ffn_W_up, L0_ffn_W_down)
    return x

_drawn_inputs = setup_inputs


def setup_inputs(seed=0):
    import zlib

    import numpy as np

    out = dict(_drawn_inputs(seed))
    spreads = {}
    factors = {'L0_xattn_wq': 3.843, 'L0_xattn_wk': 3.843}
    for name, (base, spread) in spreads.items():
        noise = np.random.default_rng([zlib.crc32(name.encode()), seed]).standard_normal(out[name].shape)
        drawn = base * np.exp(spread * noise) if base else spread * noise
        out[name] = jnp.asarray(drawn.astype(out[name].dtype))
    for name, factor in factors.items():
        out[name] = (out[name] * factor).astype(out[name].dtype)
    return out
```

```python
from contextlib import ExitStack

import concourse.bass as bass
from concourse import mybir

P = 128
F32 = mybir.dt.float32
F32R = mybir.dt.float32r
ALU = mybir.AluOpType
ACT = mybir.ActivationFunctionType
AX_X = mybir.AxisListType.X
LN_EPS = 1e-5
MASKED = -1e9
NO_BOUND = 3e38


def gated_cross_attention_block(
    nc: bass.Bass,
    x: bass.AP,
    ctx_t: bass.AP,
    mask: bass.AP,
    gates: bass.AP,
    wq: bass.AP,
    wkv: bass.AP,
    wo: bass.AP,
    w_ffn: bass.AP,
    rope: bass.AP,
    ident: bass.AP,
    out: bass.AP,
):
    B, S, DM = x.shape
    KC = DM // P
    G = wq.shape[0]
    HPG = wo.shape[2] // DM
    FC = w_ffn.shape[0]
    HALF = B // 2
    ROWS = HALF * S
    UNITS = G * B
    GU = KC * 2 * P
    assert S == P and ROWS == 512 and DM == 512 and HPG * P == 512 and B == 8 and FC % 2 == 1

    with ExitStack() as ctx:
        def sb(name, shape, dt=F32):
            return ctx.enter_context(nc.sbuf_tensor(name, shape, dt))

        def sem(name):
            return ctx.enter_context(nc.semaphore(name))

        xn_hi = sb("xn_hi", [P, 2, KC, ROWS], F32R)
        xn_lo = sb("xn_lo", [P, 2, KC, ROWS], F32R)
        c_hi = sb("c_hi", [P, B * KC * P], F32R)
        c_lo = sb("c_lo", [P, B * KC * P], F32R)
        wq_hi = sb("wq_hi", [P, HPG, KC, P], F32R)
        wq_lo = sb("wq_lo", [P, HPG, KC, P], F32R)
        wkv_hi = sb("wkv_hi", [P, KC, 2 * P], F32R)
        wkv_lo = sb("wkv_lo", [P, KC, 2 * P], F32R)
        wo_hi = sb("wo_hi", [P, HPG, DM], F32R)
        wo_lo = sb("wo_lo", [P, HPG, DM], F32R)
        v_hi = sb("v_hi", [P, B, P], F32R)
        v_lo = sb("v_lo", [P, B, P], F32R)
        pt_hi = sb("pt_hi", [P, HPG * P], F32R)
        pt_lo = sb("pt_lo", [P, HPG * P], F32R)
        ot_hi = sb("ot_hi", [P, HPG * P], F32R)
        ot_lo = sb("ot_lo", [P, HPG * P], F32R)

        acc = sb("acc", [P, B, DM])
        wq_raw = sb("wq_raw", [P, HPG * KC * P])
        wkv_raw = sb("wkv_raw", [P, KC * 2 * P])
        wo_raw = sb("wo_raw", [P, HPG * DM])
        q_rot = sb("q_rot", [P, 2, HPG, ROWS])
        k_rot = sb("k_rot", [P, B, P])
        k_rows = sb("k_rows", [P, P])
        bound = sb("bound", [P, B, S])
        tables = sb("tables", [P, 4, P])
        cos_q, sin_q, cos_k, sin_k = (tables[:, n, :] for n in range(4))
        idn = sb("idn", [P, P])
        q_swap = sb("q_swap", [P, ROWS])
        q_c = sb("q_c", [P, ROWS])
        q_s = sb("q_s", [P, ROWS])
        k_c = sb("k_c", [P, P])
        k_s = sb("k_s", [P, P])
        prob = sb("prob", [P, 2, HPG, P])
        xn = sb("xn", [P, DM])
        nmax = sb("nmax", [P, 2, HPG])
        rsum = sb("rsum", [P, 2, HPG])
        rinv = sb("rinv", [P, 2, HPG])
        stats = sb("stats", [P, B, 6])
        meanvar = sb("meanvar", [P, B, 2])
        vareps = sb("vareps", [P, B])
        rstd = sb("rstd", [P, B])
        minus_half = sb("minus_half", [P, B])
        gate_in = sb("gate_in", [P, 2])
        gate_tanh = sb("gate_tanh", [P, 2])

        bank = [ctx.enter_context(nc.psum_tensor(f"bank{n}", [P, 512], F32)) for n in range(8)]
        ps_q = [bank[0], bank[1]]
        ps_kv = bank[2][:, 0:2 * P]
        ps_s, ps_pt, ps_o, ps_wo = bank[3], bank[4], bank[5], bank[6]
        ps_kt = bank[7][:, 0:P]
        ps_x = [bank[6], bank[7]]
        ps_gate = [bank[0], bank[1]]
        ps_up = [bank[4], bank[5]]
        ps_y = [bank[2], bank[3], bank[6], bank[7]]

        fw_raw = [wq_raw, wo_raw]
        FW = GU + DM
        fw_hi = [c_hi[:, n * FW:(n + 1) * FW] for n in range(2)]
        fw_lo = [c_lo[:, n * FW:(n + 1) * FW] for n in range(2)]
        silu = [q_c, q_s]
        hid = [prob[:, n, :, :].rearrange("p h k -> p (h k)") for n in range(2)]
        hid_hi = [pt_hi, ot_hi]
        hid_lo = [pt_lo, ot_lo]

        consts_in = sem("consts_in")
        x_in = [sem(f"x_in{b}") for b in range(B)]
        c_in = [sem(f"c_in{b}") for b in range(B)]
        mask_in, gates_in = sem("mask_in"), sem("gates_in")
        wq_in, wkv_in, wo_in = sem("wq_in"), sem("wkv_in"), sem("wo_in")
        fw_in = [sem("fw_in0"), sem("fw_in1")]
        out_stored = sem("out_stored")
        c_hi_ok, c_lo_ok = sem("c_hi_ok"), sem("c_lo_ok")
        wq_hi_ok, wq_lo_ok = sem("wq_hi_ok"), sem("wq_lo_ok")
        wkv_hi_ok, wkv_lo_ok = sem("wkv_hi_ok"), sem("wkv_lo_ok")
        wo_hi_ok, wo_lo_ok = sem("wo_hi_ok"), sem("wo_lo_ok")
        ln_stats, ln_aggr, ln_var, ln_rstd, ln_rows = (sem(n) for n in ("ln_stats", "ln_aggr", "ln_var", "ln_rstd", "ln_rows"))
        half_ok = sem("half_ok")
        xt_done, xn_hi_ok, xn_lo_ok = sem("xt_done"), sem("xn_hi_ok"), sem("xn_lo_ok")
        bound_cmp, bound_ok, tanh_ok = sem("bound_cmp"), sem("bound_ok"), sem("tanh_ok")
        q_done, q_swap_ok, q_cos_ok, q_sin_ok, q_rot_ok = (
            sem(n) for n in ("q_done", "q_swap_ok", "q_cos_ok", "q_sin_ok", "q_rot_ok"))
        kv_done, k_cos_ok, k_sin_ok, k_rows_ok, kt_done, k_rot_ok = (
            sem(n) for n in ("kv_done", "k_cos_ok", "k_sin_ok", "k_rows_ok", "kt_done", "k_rot_ok"))
        v_hi_ok, v_lo_ok = sem("v_hi_ok"), sem("v_lo_ok")
        s_done, s_bound_ok, s_max_ok, exp_ok, rinv_ok, prob_ok = (
            sem(n) for n in ("s_done", "s_bound_ok", "s_max_ok", "exp_ok", "rinv_ok", "prob_ok"))
        pt_done, pt_hi_ok, pt_lo_ok = sem("pt_done"), sem("pt_hi_ok"), sem("pt_lo_ok")
        o_done, ot_hi_ok, ot_lo_ok = sem("o_done"), sem("ot_hi_ok"), sem("ot_lo_ok")
        wo_done, acc_ok = sem("wo_done"), sem("acc_ok")
        gu_hi_ok, gu_lo_ok, dn_hi_ok, dn_lo_ok = (sem(n) for n in ("gu_hi_ok", "gu_lo_ok", "dn_hi_ok", "dn_lo_ok"))
        gate_done, up_done, silu_ok, hid_ok, hid_hi_ok, hid_lo_ok, down_done, y_ok = (
            sem(n) for n in ("gate_done", "up_done", "silu_ok", "hid_ok", "hid_hi_ok", "hid_lo_ok", "down_done", "y_ok"))

        LEAD_Q = HALF + 1
        LEAD_KV = HALF

        def f32(ap):
            return ap.bitcast(F32)

        def c_part(t, b):
            return t[:, b * KC * P:(b + 1) * KC * P]

        def xn_part(t, b):
            return t[:, b // HALF, :, (b % HALF) * P:(b % HALF + 1) * P]

        def chunks(ap):
            return ap.rearrange("p (k r) -> p k r", k=KC)

        def heads(ap):
            return ap.rearrange("p (h r) -> p h r", h=HPG)

        def over_heads(ap):
            return ap.unsqueeze(1).broadcast_to([P, HPG, P])

        def attention_slots(engine, slot):
            with engine.Fori(0, G - 1) as g:
                for b in range(B):
                    slot(g, b, False)
            for b in range(B):
                slot(G - 1, b, True)

        def mlp_steps(engine, step):
            for half in range(2):
                step(0, half, 0)
                with engine.Fori(0, (FC - 3) // 2) as i:
                    for j in (1, 2):
                        step(i, half, j)
                for f in (FC - 2, FC - 1):
                    step(0, half, f)

        def fw_loads(i, t0):
            return (i + (t0 // 2 + 1)) * 16

        block = ctx.enter_context(nc.Block())

        @block.sync
        def _(sp):
            def load_c(b):
                sp.dma_start(q_rot[:, b // HALF, b % HALF, :], ctx_t[b].rearrange("p k r -> p (k r)")).then_inc(c_in[b], 16)

            load_c(0)
            sp.dma_start(wkv_raw[:, :], wkv[0]).then_inc(wkv_in, 16)
            sp.dma_start(acc[:, 0, :], x[0]).then_inc(x_in[0], 16)
            sp.dma_start(idn[:, :], ident).then_inc(consts_in, 16)
            sp.dma_start(tables[:, :, :], rope.rearrange("n p r -> p n r")).then_inc(consts_in, 16)
            for b in range(1, HALF):
                load_c(b)
                sp.dma_start(acc[:, b, :], x[b]).then_inc(x_in[b], 16)
            sp.dma_start(wq_raw[:, :], wq[0]).then_inc(wq_in, 16)
            sp.dma_start(bound[:, :, :], mask).then_inc(mask_in, 16)
            for b in range(HALF, B):
                sp.dma_start(acc[:, b, :], x[b]).then_inc(x_in[b], 16)
                load_c(b)
            sp.dma_start(gate_in[:, :], gates).then_inc(gates_in, 16)
            sp.dma_start(wo_raw[:, :], wo[0]).then_inc(wo_in, 16)
            with sp.Fori(0, G - 1) as g:
                sp.wait_ge(wq_hi_ok, g * HPG + HPG)
                sp.wait_ge(wq_lo_ok, g * HPG + HPG)
                sp.dma_start(wq_raw[:, :], wq[g + 1]).then_inc(wq_in, 16)
                sp.wait_ge(wkv_hi_ok, g + 1)
                sp.wait_ge(wkv_lo_ok, g + 1)
                sp.dma_start(wkv_raw[:, :], wkv[g + 1]).then_inc(wkv_in, 16)
                sp.wait_ge(wo_hi_ok, g * HPG + HPG)
                sp.wait_ge(wo_lo_ok, g * HPG + HPG)
                sp.dma_start(wo_raw[:, :], wo[g + 1]).then_inc(wo_in, 16)
            sp.wait_ge(wq_hi_ok, G * HPG)
            sp.wait_ge(wq_lo_ok, G * HPG)
            sp.dma_start(fw_raw[0][:, 0:FW], w_ffn[0]).then_inc(fw_in[0], 16)
            sp.wait_ge(wo_hi_ok, G * HPG)
            sp.wait_ge(wo_lo_ok, G * HPG)
            sp.dma_start(fw_raw[1][:, 0:FW], w_ffn[1]).then_inc(fw_in[1], 16)

            def load_fw(t, f, par):
                sp.wait_ge(dn_hi_ok, t - 1)
                sp.wait_ge(dn_lo_ok, t - 1)
                sp.wait_ge(gu_hi_ok, t - 1)
                sp.wait_ge(gu_lo_ok, t - 1)
                sp.dma_start(fw_raw[par][:, 0:FW], w_ffn[f]).then_inc(fw_in[par], 16)

            def store(half):
                for j in range(HALF):
                    b = half * HALF + j
                    sp.wait_ge(y_ok, b + 1)
                    sp.dma_start(out[b], acc[:, b, :]).then_inc(out_stored, 16)

            with sp.Fori(0, (FC - 3) // 2) as i:
                for j in (0, 1):
                    load_fw(i * 2 + (2 + j), i * 2 + (2 + j), j)
            load_fw(FC - 1, FC - 1, (FC - 1) % 2)
            for f in range(2):
                load_fw(FC + f, f, (FC + f) % 2)
            store(0)
            with sp.Fori(0, (FC - 3) // 2) as i:
                for j in (0, 1):
                    load_fw(i * 2 + (FC + 2 + j), i * 2 + (2 + j), (FC + j) % 2)
            load_fw(2 * FC - 1, FC - 1, (2 * FC - 1) % 2)
            store(1)
            sp.wait_ge(out_stored, 16 * B)

        @block.tensor
        def _(pe):
            def product(out_ps, lhs, rhs, first=True, last=True):
                (lh, ll), (rh, rl) = lhs, rhs
                pe.matmul(out_ps, lh, rh, start=first, stop=False)
                pe.matmul(out_ps, lh, rl, start=False, stop=False)
                return pe.matmul(out_ps, ll, rh, start=False, stop=last)

            def transpose_xn(b, total):
                pe.wait_ge(ln_rows, total + 1)
                if total > 0:
                    pe.wait_ge(xn_lo_ok, total)
                if total >= B:
                    pe.wait_ge(k_rot_ok, UNITS - B + min(b + 5, B))
                for k in range(KC):
                    mm = pe.transpose(ps_x[total // B][:, k * P:(k + 1) * P], xn[:, k * P:(k + 1) * P], idn[:, :])
                mm.then_inc(xt_done, 1)

            def project_q(n, head, half, ps, parts):
                for k in parts:
                    mm = product(ps[:, :], (wq_hi[:, head, k, :], wq_lo[:, head, k, :]),
                                 (xn_hi[:, half, k, :], xn_lo[:, half, k, :]), k == 0, k == KC - 1)
                if KC - 1 in parts:
                    mm.then_inc(q_done, 1)

            def project_kv(b):
                for k in range(KC):
                    c = slice((b * KC + k) * P, (b * KC + k + 1) * P)
                    mm = product(ps_kv, (c_hi[:, c], c_lo[:, c]), (wkv_hi[:, k, :], wkv_lo[:, k, :]),
                                 k == 0, k == KC - 1)
                mm.then_inc(kv_done, 1)

            def scores(b):
                for h in range(HPG):
                    q = q_rot[:, b // HALF, h, (b % HALF) * P:(b % HALF + 1) * P]
                    mm = pe.matmul(ps_s[:, h * P:(h + 1) * P], q, k_rot[:, b, :], start=True, stop=True)
                mm.then_inc(s_done, 1)

            pe.wait_ge(consts_in, 32)
            for n in range(LEAD_KV):
                pe.wait_ge(c_hi_ok, n + 1)
                pe.wait_ge(c_lo_ok, n + 1)
                if n == 0:
                    pe.wait_ge(wkv_hi_ok, 1)
                    pe.wait_ge(wkv_lo_ok, 1)
                else:
                    pe.wait_ge(v_lo_ok, n)
                project_kv(n)
                transpose_xn(n, n)
                if n > 0:
                    pe.wait_ge(k_rows_ok, n)
                    if n > 1:
                        pe.wait_ge(k_rot_ok, n - 1)
                    pe.transpose(ps_kt, k_rows[:, :], idn[:, :]).then_inc(kt_done, 1)
            pe.wait_ge(xn_hi_ok, HALF)
            pe.wait_ge(xn_lo_ok, HALF)
            for n in range(HPG):
                pe.wait_ge(wq_hi_ok, n + 1)
                pe.wait_ge(wq_lo_ok, n + 1)
                if n >= 2:
                    pe.wait_ge(q_cos_ok, n - 1)
                project_q(n, n, 0, ps_q[n % 2], range(KC))
                transpose_xn(HALF + n, HALF + n)
            pe.wait_ge(q_rot_ok, HPG)
            pe.wait_ge(k_rot_ok, 1)
            scores(0)
            pe.wait_ge(xn_hi_ok, B)
            pe.wait_ge(xn_lo_ok, B)
            pe.wait_ge(c_hi_ok, B)
            pe.wait_ge(c_lo_ok, B)
            pe.wait_ge(q_cos_ok, HPG - 1)
            project_q(HPG, 0, 1, ps_q[HPG % 2], range(KC))

            def slot(g, b, last):
                u = g * B
                pe.wait_ge(prob_ok, u + (b + 1))
                for h in range(HPG):
                    mm = pe.transpose(ps_pt[:, h * P:(h + 1) * P], prob[:, b % 2, h, :], idn[:, :])
                mm.then_inc(pt_done, 1)
                if not (last and b == B - 1):
                    nb = (b + 1) % B
                    pe.wait_ge(q_rot_ok, u + (4 * ((b + 1) // 4) + 4))
                    pe.wait_ge(k_rot_ok, u + (b + 2))
                    scores(nb)
                n = b + LEAD_Q
                project = not last or n < B
                if project:
                    if n >= B:
                        pe.wait_ge(wq_hi_ok, g * HPG + (HPG + min(n - B, HPG - 1) + 1))
                        pe.wait_ge(wq_lo_ok, g * HPG + (HPG + min(n - B, HPG - 1) + 1))
                    pe.wait_ge(q_cos_ok, u + (n - 1))
                    where = (n, n % HPG, (n // HPG) % 2, ps_q[n % 2])
                    project_q(*where, range(0, KC // 2))
                pe.wait_ge(pt_hi_ok, u + (b + 1))
                pe.wait_ge(pt_lo_ok, u + (b + 1))
                pe.wait_ge(v_hi_ok, u + (b + 1))
                pe.wait_ge(v_lo_ok, u + (b + 1))
                product(ps_o[:, :], (v_hi[:, b, :], v_lo[:, b, :]), (pt_hi[:, :], pt_lo[:, :])).then_inc(o_done, 1)
                if project:
                    project_q(*where, range(KC // 2, KC))
                if not last or b + 3 < B:
                    pe.wait_ge(k_rows_ok, u + (b + 4))
                    pe.wait_ge(k_rot_ok, u + (b + 3))
                    if last and b > 1:
                        pe.wait_ge(xn_lo_ok, B + b - 1)
                    pe.transpose(ps_kt, k_rows[:, :], idn[:, :]).then_inc(kt_done, 1)
                n = b + LEAD_KV
                if not last or n < B:
                    if n >= B:
                        pe.wait_ge(wkv_hi_ok, g + 2)
                        pe.wait_ge(wkv_lo_ok, g + 2)
                    pe.wait_ge(v_lo_ok, u + n)
                    project_kv(n % B)
                if last and b > 0:
                    transpose_xn(b - 1, B + b - 1)
                pe.wait_ge(ot_hi_ok, u + (b + 1))
                pe.wait_ge(ot_lo_ok, u + (b + 1))
                for h in range(HPG):
                    if b == 0:
                        pe.wait_ge(wo_hi_ok, g * HPG + (h + 1))
                        pe.wait_ge(wo_lo_ok, g * HPG + (h + 1))
                    c = slice(h * P, (h + 1) * P)
                    mm = product(ps_wo[:, :], (ot_hi[:, c], ot_lo[:, c]), (wo_hi[:, h, :], wo_lo[:, h, :]),
                                 h == 0, h == HPG - 1)
                mm.then_inc(wo_done, 1)

            attention_slots(pe, slot)

            def gate_up(t, half, par):
                pe.wait_ge(gu_hi_ok, t + 1)
                pe.wait_ge(gu_lo_ok, t + 1)
                for which, ps, done in ((0, ps_gate[par], gate_done), (1, ps_up[par], up_done)):
                    for k in range(KC):
                        c = slice((which * KC + k) * P, (which * KC + k + 1) * P)
                        mm = product(ps[:, :], (fw_hi[par][:, c], fw_lo[par][:, c]),
                                     (xn_hi[:, half, k, :], xn_lo[:, half, k, :]), k == 0, k == KC - 1)
                    mm.then_inc(done, 1)

            pe.wait_ge(xn_hi_ok, B + HALF)
            pe.wait_ge(xn_lo_ok, B + HALF)
            gate_up(0, 0, 0)
            transpose_xn(B - 1, 2 * B - 1)

            def step(i, half, j):
                t0 = half * FC + j
                t, par = i * 2 + t0, t0 % 2
                first, last = j == 0, j == FC - 1
                if not (half == 1 and last):
                    if last:
                        pe.wait_ge(xn_hi_ok, 2 * B)
                        pe.wait_ge(xn_lo_ok, 2 * B)
                    if t0 > 0:
                        pe.wait_ge(silu_ok, t)
                        pe.wait_ge(hid_ok, t)
                    gate_up(t + 1, 1 if last else half, 1 - par)
                pe.wait_ge(hid_hi_ok, t + 1)
                pe.wait_ge(hid_lo_ok, t + 1)
                pe.wait_ge(dn_hi_ok, t + 1)
                pe.wait_ge(dn_lo_ok, t + 1)
                if t0 == 0:
                    pe.wait_ge(xn_lo_ok, 2 * B)
                elif first:
                    pe.wait_ge(y_ok, HALF)
                for r in range(HALF):
                    c = slice(r * P, (r + 1) * P)
                    mm = product(ps_y[r][:, :], (hid_hi[par][:, c], hid_lo[par][:, c]),
                                 (fw_hi[par][:, GU:FW], fw_lo[par][:, GU:FW]), first, last)
                mm.then_inc(down_done, 1)

            mlp_steps(pe, step)

        @block.scalar
        def _(act):
            def split_c(b):
                act.wait_ge(c_in[b], 16)
                act.activation(c_part(c_hi, b), q_rot[:, b // HALF, b % HALF, :], ACT.Copy).then_inc(c_hi_ok, 1)

            def split_wq(h, g16):
                act.wait_ge(wq_in, g16)
                act.activation(wq_hi[:, h, :, :].rearrange("p k r -> p (k r)"),
                               wq_raw[:, h * KC * P:(h + 1) * KC * P], ACT.Copy).then_inc(wq_hi_ok, 1)

            def split_wkv(g16):
                act.wait_ge(wkv_in, g16)
                act.activation(wkv_hi[:, :, :].rearrange("p k r -> p (k r)"), wkv_raw[:, :], ACT.Copy).then_inc(wkv_hi_ok, 1)

            def split_xn(b, total):
                act.wait_ge(xt_done, total + 1)
                act.activation(xn_part(xn_hi, b), chunks(ps_x[total // B][:, :]), ACT.Copy).then_inc(xn_hi_ok, 1)

            def swap_q(ps, nq):
                act.wait_ge(q_done, nq + 1)
                act.wait_ge(q_sin_ok, nq)
                act.activation(q_swap[0:P // 2, :], ps[P // 2:P, :], ACT.Copy)
                act.activation(q_swap[P // 2:P, :], ps[0:P // 2, :], ACT.Copy).then_inc(q_swap_ok, 1)

            def take_v(b, n):
                act.wait_ge(kv_done, n + 1)
                act.activation(v_hi[:, b, :], ps_kv[:, P:2 * P], ACT.Copy).then_inc(v_hi_ok, 1)

            def take_kt(b, n):
                act.wait_ge(kt_done, n + 1)
                act.activation(k_rot[:, b, :], ps_kt, ACT.Copy).then_inc(k_rot_ok, 1)

            def exponentials(par, n):
                act.wait_ge(s_max_ok, n + 1)
                for h in range(HPG):
                    e = act.activation(prob[:, par, h, :], ps_s[:, h * P:(h + 1) * P], ACT.Exp,
                                       bias=nmax[:, par, h:h + 1], scale=-1.0, accum_out=rsum[:, par, h:h + 1])
                e.then_inc(exp_ok, 1)

            split_c(0)
            split_wkv(16)
            take_v(0, 0)
            for b in range(1, HALF):
                split_c(b)
                split_xn(b - 1, b - 1)
                take_v(b, b)
                if b > 1:
                    take_kt(b - 2, b - 2)
            split_xn(HALF - 1, HALF - 1)
            take_kt(HALF - 2, HALF - 2)
            for h in range(HPG):
                split_wq(h, 16)
            for b in range(HALF, B):
                split_c(b)
                swap_q(ps_q[b % 2], b - HALF)
                split_xn(b, b)
            act.wait_ge(gates_in, 16)
            act.activation(gate_tanh[:, :], gate_in[:, :], ACT.Tanh).then_inc(tanh_ok, 1)
            exponentials(0, 0)
            swap_q(ps_q[HPG % 2], HPG)

            def split_gu(par, loaded):
                act.wait_ge(fw_in[par], loaded)
                act.activation(fw_hi[par][:, 0:GU], fw_raw[par][:, 0:GU], ACT.Copy).then_inc(gu_hi_ok, 1)

            def slot(g, b, last):
                u = g * B
                act.wait_ge(pt_done, u + (b + 1))
                act.activation(pt_hi[:, :], ps_pt[:, :], ACT.Copy).then_inc(pt_hi_ok, 1)
                if b == 0:
                    act.wait_ge(wo_in, g * 16 + 16)
                    for h in range(HPG):
                        act.activation(wo_hi[:, h, :], wo_raw[:, h * DM:(h + 1) * DM], ACT.Copy).then_inc(wo_hi_ok, 1)
                if not (last and b == B - 1):
                    exponentials((b + 1) % 2, u + (b + 1))
                act.wait_ge(o_done, u + (b + 1))
                act.activation(ot_hi[:, :], ps_o[:, :], ACT.Copy).then_inc(ot_hi_ok, 1)
                n = b + LEAD_Q
                if not last or n < B:
                    swap_q(ps_q[n % 2], u + n)
                if not last or b + 3 < B:
                    take_kt((b + 3) % B, u + (b + 3))
                n = b + LEAD_KV
                if not last or n < B:
                    take_v(n % B, u + n)
                if not last:
                    if 1 <= b <= HPG:
                        split_wq(b - 1, g * 16 + 32)
                    if b == HALF - 1:
                        split_wkv(g * 16 + 32)
                else:
                    if b > 0:
                        split_xn(b - 1, B + b - 1)
                    if b == HALF:
                        split_gu(0, 16)

            attention_slots(act, slot)

            def step(i, half, j):
                t0 = half * FC + j
                t, par = i * 2 + t0, t0 % 2
                act.wait_ge(gate_done, t + 1)
                act.activation(silu[par][:, :], ps_gate[par][:, :], ACT.Silu).then_inc(silu_ok, 1)
                if t0 == 0:
                    split_xn(B - 1, 2 * B - 1)
                if t0 != 2 * FC - 1:
                    split_gu(1 - par, fw_loads(i, t0 + 1))
                act.activation(fw_hi[par][:, GU:FW], fw_raw[par][:, GU:FW], ACT.Copy).then_inc(dn_hi_ok, 1)
                act.wait_ge(hid_ok, t + 1)
                act.activation(hid_hi[par][:, :], hid[par], ACT.Copy).then_inc(hid_hi_ok, 1)

            mlp_steps(act, step)

        @block.vector
        def _(dve):
            def sub(out_lo, whole, hi):
                return dve.tensor_tensor(out_lo, whole, f32(hi), ALU.subtract)

            def ln_stat(b, total):
                dve.bn_stats(stats[:, b, :], acc[:, b, :]).then_inc(ln_stats, 1)
                dve.wait_ge(ln_stats, total + 1)
                dve.bn_aggr(meanvar[:, b, :], stats[:, b, :]).then_inc(ln_aggr, 1)
                dve.wait_ge(ln_aggr, total + 1)
                dve.tensor_scalar(vareps[:, b:b + 1], meanvar[:, b, 1:2], LN_EPS, None, ALU.add).then_inc(ln_var, 1)

            def ln_row(b, total):
                dve.wait_ge(ln_rstd, total + 1)
                dve.wait_ge(xt_done, total)
                dve.tensor_scalar(xn[:, :], acc[:, b, :], meanvar[:, b, 0:1], rstd[:, b:b + 1],
                                  ALU.subtract, ALU.mult).then_inc(ln_rows, 1)

            def split_xn(b, total):
                dve.wait_ge(xn_hi_ok, total + 1)
                sub(xn_part(xn_lo, b), chunks(ps_x[total // B][:, :]), xn_part(xn_hi, b)).then_inc(xn_lo_ok, 1)

            def rope_k(n):
                dve.wait_ge(v_hi_ok, n + 1)
                dve.tensor_tensor(k_c[:, :], ps_kv[:, 0:P], cos_k, ALU.mult).then_inc(k_cos_ok, 1)
                lo, up = slice(0, P // 2), slice(P // 2, P)
                dve.tensor_tensor(k_s[:, lo], ps_kv[:, up], sin_k[:, lo], ALU.mult)
                dve.tensor_tensor(k_s[:, up], ps_kv[:, lo], sin_k[:, up], ALU.mult).then_inc(k_sin_ok, 1)
                dve.wait_ge(k_cos_ok, n + 1)
                dve.wait_ge(k_sin_ok, n + 1)
                dve.wait_ge(kt_done, n)
                dve.tensor_tensor(k_rows[:, :], k_c[:, :], k_s[:, :], ALU.add).then_inc(k_rows_ok, 1)

            def split_v(b, n):
                sub(v_lo[:, b, :], ps_kv[:, P:2 * P], v_hi[:, b, :]).then_inc(v_lo_ok, 1)

            def split_wkv(count):
                dve.wait_ge(wkv_hi_ok, count)
                sub(wkv_lo[:, :, :].rearrange("p k r -> p (k r)"), wkv_raw[:, :],
                    wkv_hi[:, :, :].rearrange("p k r -> p (k r)")).then_inc(wkv_lo_ok, 1)

            def rope_q(ps, n):
                dve.wait_ge(q_swap_ok, n + 1)
                dve.wait_ge(q_rot_ok, n)
                dve.tensor_tensor(heads(q_c[:, :]), heads(ps[:, :]), over_heads(cos_q), ALU.mult).then_inc(q_cos_ok, 1)
                dve.tensor_tensor(heads(q_s[:, :]), heads(q_swap[:, :]), over_heads(sin_q), ALU.mult).then_inc(q_sin_ok, 1)

            def row_max(b, par, n):
                dve.wait_ge(s_done, n + 1)
                dve.tensor_tensor(heads(ps_s[:, :]), heads(ps_s[:, :]), over_heads(bound[:, b, :]),
                                  ALU.max).then_inc(s_bound_ok, 1)
                dve.wait_ge(s_bound_ok, n + 1)
                dve.tensor_reduce(nmax[:, par, :], heads(ps_s[:, :]), AX_X, ALU.min).then_inc(s_max_ok, 1)

            def invert_sums(par, n):
                dve.wait_ge(exp_ok, n + 1)
                dve.reciprocal(rinv[:, par, :], rsum[:, par, :]).then_inc(rinv_ok, 1)

            dve.wait_ge(x_in[0], 16)
            ln_stat(0, 0)
            split_wkv(1)
            ln_row(0, 0)
            dve.wait_ge(consts_in, 32)
            for b in range(HALF):
                rope_k(b)
                split_v(b, b)
                split_xn(b, b)
                dve.wait_ge(x_in[b + 1], 16)
                ln_stat(b + 1, b + 1)
                ln_row(b + 1, b + 1)
            for b in range(HALF, B):
                rope_q(ps_q[b % 2], b - HALF)
                split_xn(b, b)
                if b + 1 < B:
                    dve.wait_ge(x_in[b + 1], 16)
                    ln_stat(b + 1, b + 1)
                    ln_row(b + 1, b + 1)
            dve.wait_ge(mask_in, 16)
            dve.tensor_scalar(bound[:, :, :], bound[:, :, :], 0.0, None, ALU.not_equal).then_inc(bound_cmp, 1)
            dve.wait_ge(bound_cmp, 1)
            dve.tensor_scalar(bound[:, :, :], bound[:, :, :], -NO_BOUND, -MASKED, ALU.mult, ALU.add).then_inc(bound_ok, 1)
            dve.wait_ge(bound_ok, 1)
            dve.wait_ge(tanh_ok, 1)
            row_max(0, 0, 0)
            invert_sums(0, 0)
            rope_q(ps_q[HPG % 2], HPG)

            def slot(g, b, last):
                u = g * B
                dve.wait_ge(pt_hi_ok, u + (b + 1))
                sub(pt_lo[:, :], ps_pt[:, :], pt_hi[:, :]).then_inc(pt_lo_ok, 1)
                more = not (last and b == B - 1)
                if more:
                    row_max((b + 1) % B, (b + 1) % 2, u + (b + 1))
                if last and b > 0:
                    dve.wait_ge(acc_ok, u + b)
                    ln_stat(b - 1, B + b - 1)
                dve.wait_ge(ot_hi_ok, u + (b + 1))
                sub(ot_lo[:, :], ps_o[:, :], ot_hi[:, :]).then_inc(ot_lo_ok, 1)
                if more:
                    invert_sums((b + 1) % 2, u + (b + 1))
                if last and b > 0:
                    ln_row(b - 1, B + b - 1)
                n = b + LEAD_Q
                if not last or n < B:
                    rope_q(ps_q[n % 2], u + n)
                n = b + LEAD_KV
                if not last or n < B:
                    rope_k(u + n)
                    split_v(n % B, u + n)
                if not last and b == HALF - 1:
                    split_wkv(g + 2)
                if last and b > 0:
                    split_xn(b - 1, B + b - 1)
                dve.wait_ge(wo_done, u + (b + 1))
                dve.scalar_tensor_tensor(out=acc[:, b, :], in0=ps_wo[:, :], scalar=gate_tanh[:, 0:1],
                                         in1=acc[:, b, :], op0=ALU.mult, op1=ALU.add).then_inc(acc_ok, 1)

            attention_slots(dve, slot)
            dve.wait_ge(acc_ok, UNITS)
            ln_stat(B - 1, 2 * B - 1)
            ln_row(B - 1, 2 * B - 1)

            def step(i, half, j):
                t0 = half * FC + j
                t, par = i * 2 + t0, t0 % 2
                dve.wait_ge(silu_ok, t + 1)
                dve.wait_ge(up_done, t + 1)
                dve.tensor_tensor(hid[par], ps_up[par][:, :], silu[par][:, :], ALU.mult).then_inc(hid_ok, 1)
                if t0 == 0:
                    split_xn(B - 1, 2 * B - 1)
                dve.wait_ge(hid_hi_ok, t + 1)
                sub(hid_lo[par][:, :], hid[par], hid_hi[par][:, :]).then_inc(hid_lo_ok, 1)
                if j == FC - 1:
                    dve.wait_ge(down_done, t + 1)
                    for r in range(HALF):
                        b = half * HALF + r
                        dve.scalar_tensor_tensor(out=acc[:, b, :], in0=ps_y[r][:, :], scalar=gate_tanh[:, 1:2],
                                                 in1=acc[:, b, :], op0=ALU.mult, op1=ALU.add).then_inc(y_ok, 1)

            mlp_steps(dve, step)

        @block.gpsimd
        def _(pool):
            def sub(out_lo, whole, hi):
                return pool.tensor_tensor(out_lo, whole, f32(hi), ALU.subtract)

            def split_c(b):
                pool.wait_ge(c_hi_ok, b + 1)
                sub(c_part(c_lo, b), q_rot[:, b // HALF, b % HALF, :], c_part(c_hi, b)).then_inc(c_lo_ok, 1)

            def ln_power(b, total):
                pool.wait_ge(ln_var, total + 1)
                pool.tensor_tensor(rstd[:, b:b + 1], vareps[:, b:b + 1], minus_half[:, b:b + 1],
                                   ALU.pow).then_inc(ln_rstd, 1)

            def split_wq(h, count):
                pool.wait_ge(wq_hi_ok, count)
                sub(wq_lo[:, h, :, :].rearrange("p k r -> p (k r)"), wq_raw[:, h * KC * P:(h + 1) * KC * P],
                    wq_hi[:, h, :, :].rearrange("p k r -> p (k r)")).then_inc(wq_lo_ok, 1)

            def add_q(half, head, n):
                pool.wait_ge(q_cos_ok, n + 1)
                pool.wait_ge(q_sin_ok, n + 1)
                pool.tensor_tensor(q_rot[:, half, head, :], q_c[:, :], q_s[:, :], ALU.add).then_inc(q_rot_ok, 1)

            def normalise(par, n):
                pool.wait_ge(rinv_ok, n + 1)
                p4 = prob[:, par, :, :]
                pool.tensor_tensor(p4, p4, rinv[:, par, :].unsqueeze(2).broadcast_to([P, HPG, P]),
                                   ALU.mult).then_inc(prob_ok, 1)

            pool.memset(minus_half[:, :], -0.5).then_inc(half_ok, 1)
            pool.wait_ge(half_ok, 1)
            for b in range(HALF):
                split_c(b)
                ln_power(b, b)
            for h in range(HPG):
                split_wq(h, h + 1)
            for b in range(HALF, B):
                ln_power(b, b)
                add_q(0, b - HALF, b - HALF)
                split_c(b)
            normalise(0, 0)
            add_q(1, 0, HPG)

            def split_gu(t, par):
                pool.wait_ge(gu_hi_ok, t + 1)
                sub(fw_lo[par][:, 0:GU], fw_raw[par][:, 0:GU], fw_hi[par][:, 0:GU]).then_inc(gu_lo_ok, 1)

            def slot(g, b, last):
                u = g * B
                if b == 0:
                    for h in range(HPG):
                        pool.wait_ge(wo_hi_ok, g * HPG + (h + 1))
                        sub(wo_lo[:, h, :], wo_raw[:, h * DM:(h + 1) * DM], wo_hi[:, h, :]).then_inc(wo_lo_ok, 1)
                if last and b > 0:
                    ln_power(b - 1, B + b - 1)
                if not (last and b == B - 1):
                    normalise((b + 1) % 2, u + (b + 1))
                n = b + LEAD_Q
                if not last or n < B:
                    add_q((n // HPG) % 2, n % HPG, u + n)
                if not last and 1 <= b <= HPG:
                    split_wq(b - 1, g * HPG + (HPG + b))
                if last and b == HALF:
                    split_gu(0, 0)

            attention_slots(pool, slot)
            ln_power(B - 1, 2 * B - 1)

            def step(i, half, j):
                t0 = half * FC + j
                t, par = i * 2 + t0, t0 % 2
                if t0 != 2 * FC - 1:
                    split_gu(t + 1, 1 - par)
                pool.wait_ge(dn_hi_ok, t + 1)
                sub(fw_lo[par][:, GU:FW], fw_raw[par][:, GU:FW], fw_hi[par][:, GU:FW]).then_inc(dn_lo_ok, 1)

            mlp_steps(pool, step)


def rope_tables(n_rows, dim, np):
    inv_freq = 1.0 / np.float32(10000.0) ** (np.arange(0, dim, 2, dtype=np.float32) / np.float32(dim))
    ang = np.arange(n_rows, dtype=np.float32)[:, None] * inv_freq[None, :].astype(np.float32)
    cos, sin = np.cos(ang), np.sin(ang)
    cos = np.concatenate([cos, cos], axis=1)
    sin = np.concatenate([-sin, sin], axis=1)
    by = -1.0 / np.sqrt(np.float64(dim))
    return np.stack([cos.T * by, sin.T * by, cos, sin]).astype(np.float32)


def kernel(x, ctx_4096, mask_BxSxS2_ff1, g_xattn, g_ffn, L0_xattn_wq, L0_xattn_wk, L0_xattn_wv, L0_xattn_wo,
           L0_ffn_W_gate, L0_ffn_W_up, L0_ffn_W_down):
    import numpy as np
    import concourse.bacc as bacc
    from concourse.bass_utils import run_bass_kernel_spmd

    x, c, mask, g_x, g_f, wq, wk, wv, wo, w_gate, w_up, w_down = (
        np.asarray(a) for a in (x, ctx_4096, mask_BxSxS2_ff1, g_xattn, g_ffn, L0_xattn_wq, L0_xattn_wk,
                                L0_xattn_wv, L0_xattn_wo, L0_ffn_W_gate, L0_ffn_W_up, L0_ffn_W_down))
    B, S, DM = x.shape
    KC, G = DM // P, wk.shape[1] // P
    HPG = wq.shape[1] // (G * P)
    F = w_gate.shape[0]
    FC = -(-F // P)
    pad = FC * P - F

    def kcols(w, heads):
        return w.reshape(KC, P, G, heads, P).transpose(2, 1, 3, 0, 4)

    def chunked(w):
        return np.pad(w, ((0, pad), (0, 0))).reshape(FC, P, KC, P).transpose(0, 3, 2, 1)

    wkv = np.concatenate([kcols(wk, 1)[:, :, 0], kcols(wv, 1)[:, :, 0]], axis=3)
    down = np.pad(w_down.T, ((0, pad), (0, 0))).reshape(FC, P, DM)
    w_ffn = np.concatenate([chunked(w_gate).reshape(FC, P, KC * P), chunked(w_up).reshape(FC, P, KC * P), down], axis=2)
    gates = np.empty((P, 2), x.dtype)
    gates[:, 0], gates[:, 1] = g_x[0], g_f[0]
    arrays = {
        "x": x,
        "ctx_t": c.reshape(B, S, KC, P).transpose(0, 3, 2, 1),
        "mask": mask.transpose(1, 0, 2),
        "gates": gates,
        "wq": kcols(wq, HPG).reshape(G, P, HPG * KC * P),
        "wkv": wkv.reshape(G, P, KC * 2 * P),
        "wo": wo.reshape(G, HPG, P, DM).transpose(0, 2, 1, 3).reshape(G, P, HPG * DM),
        "w_ffn": w_ffn,
        "rope": rope_tables(S, P, np),
        "ident": np.eye(P, dtype=np.float32),
    }
    arrays = {f"in_{n}": np.ascontiguousarray(a) for n, a in arrays.items()}
    nc = bacc.Bacc("TRN2", target_bir_lowering=False, num_devices=1)
    ins = [nc.dram_tensor(n, a.shape, mybir.dt.from_np(a.dtype), kind="ExternalInput").ap() for n, a in arrays.items()]
    out = nc.dram_tensor("out_0", (B, S, DM), F32, kind="ExternalOutput").ap()
    gated_cross_attention_block(nc, *ins, out)
    r = run_bass_kernel_spmd(nc, [arrays], core_ids=[0])
    return r.results[0]["out_0"]
```

```python
from contextlib import ExitStack

import concourse.bass as bass
from concourse import mybir

P = 128
F32 = mybir.dt.float32
F32R = mybir.dt.float32r
ALU = mybir.AluOpType
ACT = mybir.ActivationFunctionType
AX_X = mybir.AxisListType.X
LN_EPS = 1e-5
MASKED = -1e9
NO_BOUND = 3e38


def gated_cross_attention_block(
    nc: bass.Bass,
    x: bass.AP,
    ctx_t: bass.AP,
    mask: bass.AP,
    gates: bass.AP,
    wq: bass.AP,
    wkv: bass.AP,
    wo: bass.AP,
    w_ffn: bass.AP,
    rope: bass.AP,
    ident: bass.AP,
    out: bass.AP,
):
    B, S, DM = x.shape
    KC = DM // P
    G = wq.shape[0]
    HPG = wo.shape[2] // DM
    FC = w_ffn.shape[0]
    HALF = B // 2
    ROWS = HALF * S
    UNITS = G * B
    GU = KC * 2 * P
    assert S == P and ROWS == 512 and DM == 512 and HPG * P == 512 and B == 8 and FC % 2 == 1

    with ExitStack() as ctx:
        def sb(name, shape, dt=F32):
            return ctx.enter_context(nc.sbuf_tensor(name, shape, dt))

        def sem(name):
            return ctx.enter_context(nc.semaphore(name))

        xn_hi = sb("xn_hi", [P, 2, KC, ROWS], F32R)
        xn_lo = sb("xn_lo", [P, 2, KC, ROWS], F32R)
        c_hi = sb("c_hi", [P, B * KC * P], F32R)
        c_lo = sb("c_lo", [P, B * KC * P], F32R)
        wq_hi = sb("wq_hi", [P, HPG, KC, P], F32R)
        wq_lo = sb("wq_lo", [P, HPG, KC, P], F32R)
        wkv_hi = sb("wkv_hi", [P, KC, 2 * P], F32R)
        wkv_lo = sb("wkv_lo", [P, KC, 2 * P], F32R)
        wo_hi = sb("wo_hi", [P, HPG, DM], F32R)
        wo_lo = sb("wo_lo", [P, HPG, DM], F32R)
        v_hi = sb("v_hi", [P, B, P], F32R)
        v_lo = sb("v_lo", [P, B, P], F32R)
        pt_hi = sb("pt_hi", [P, HPG * P], F32R)
        pt_lo = sb("pt_lo", [P, HPG * P], F32R)
        ot_hi = sb("ot_hi", [P, HPG * P], F32R)
        ot_lo = sb("ot_lo", [P, HPG * P], F32R)

        acc = sb("acc", [P, B, DM])
        wq_raw = sb("wq_raw", [P, HPG * KC * P])
        wkv_raw = sb("wkv_raw", [P, KC * 2 * P])
        wo_raw = sb("wo_raw", [P, HPG * DM])
        q_rot = sb("q_rot", [P, 2, HPG, ROWS])
        k_rot = sb("k_rot", [P, B, P])
        k_rows = sb("k_rows", [P, P])
        bound = sb("bound", [P, B, S])
        tables = sb("tables", [P, 4, P])
        cos_q, sin_q, cos_k, sin_k = (tables[:, n, :] for n in range(4))
        idn = sb("idn", [P, P])
        q_swap = sb("q_swap", [P, ROWS])
        q_c = sb("q_c", [P, ROWS])
        q_s = sb("q_s", [P, ROWS])
        k_c = sb("k_c", [P, P])
        k_s = sb("k_s", [P, P])
        prob = sb("prob", [P, 2, HPG, P])
        xn = sb("xn", [P, 2, DM])
        nmax = sb("nmax", [P, 2, HPG])
        rsum = sb("rsum", [P, 2, HPG])
        rinv = sb("rinv", [P, 2, HPG])
        stats = sb("stats", [P, B, 6])
        meanvar = sb("meanvar", [P, B, 2])
        vareps = sb("vareps", [P, B])
        rstd = sb("rstd", [P, B])
        minus_half = sb("minus_half", [P, B])
        gate_in = sb("gate_in", [P, 2])
        gate_tanh = sb("gate_tanh", [P, 2])

        bank = [ctx.enter_context(nc.psum_tensor(f"bank{n}", [P, 512], F32)) for n in range(8)]
        ps_q = [bank[0], bank[1]]
        ps_kv = bank[2][:, 0:2 * P]
        ps_s, ps_pt, ps_o, ps_wo = bank[3], bank[4], bank[5], bank[6]
        ps_kt = bank[7][:, 0:P]
        ps_x = [[bank[6], bank[5]], [bank[7], bank[7]]]
        ps_gate = [bank[0], bank[4]]
        ps_up = [bank[1], bank[5]]
        ps_y = [bank[2], bank[3], bank[6], bank[7]]

        fw_raw = [wq_raw, wo_raw]
        FW = GU + DM
        fw_hi = [c_hi[:, n * FW:(n + 1) * FW] for n in range(2)]
        fw_lo = [c_lo[:, n * FW:(n + 1) * FW] for n in range(2)]
        silu = [q_c, q_s]
        hid = [prob[:, n, :, :].rearrange("p h k -> p (h k)") for n in range(2)]
        hid_hi = [pt_hi, ot_hi]
        hid_lo = [pt_lo, ot_lo]

        ident_in, tables_in = sem("ident_in"), sem("tables_in")
        x_in = [sem(f"x_in{b}") for b in range(B)]
        c_in = [sem(f"c_in{b}") for b in range(B)]
        mask_in, gates_in = sem("mask_in"), sem("gates_in")
        wq_in, wkv_in, wo_in = sem("wq_in"), sem("wkv_in"), sem("wo_in")
        gu_in = [sem("gu_in0"), sem("gu_in1")]
        dn_in = [sem("dn_in0"), sem("dn_in1")]
        out_stored = sem("out_stored")
        c_hi_ok, c_lo_ok, c_lo_dve_ok = sem("c_hi_ok"), sem("c_lo_ok"), sem("c_lo_dve_ok")
        wq_hi_ok, wq_lo_ok = sem("wq_hi_ok"), sem("wq_lo_ok")
        wkv_hi_ok, wkv_lo_ok = sem("wkv_hi_ok"), sem("wkv_lo_ok")
        wo_hi_ok, wo_lo_ok = sem("wo_hi_ok"), sem("wo_lo_ok")
        ln_stats, ln_aggr, ln_var, ln_rstd, ln_rows = (sem(n) for n in ("ln_stats", "ln_aggr", "ln_var", "ln_rstd", "ln_rows"))
        half_ok = sem("half_ok")
        xt_done, xn_hi_ok, xn_lo_ok = sem("xt_done"), sem("xn_hi_ok"), sem("xn_lo_ok")
        bound_cmp, bound_ok, tanh_ok = sem("bound_cmp"), sem("bound_ok"), sem("tanh_ok")
        q_done, q_swap_ok, q_cos_ok, q_sin_ok, q_rot_ok = (
            sem(n) for n in ("q_done", "q_swap_ok", "q_cos_ok", "q_sin_ok", "q_rot_ok"))
        kv_done, k_cos_ok, k_sin_ok, k_rows_ok, kt_done, k_rot_ok = (
            sem(n) for n in ("kv_done", "k_cos_ok", "k_sin_ok", "k_rows_ok", "kt_done", "k_rot_ok"))
        v_hi_ok, v_lo_ok = sem("v_hi_ok"), sem("v_lo_ok")
        s_done, s_bound_ok, s_max_ok, exp_ok, rinv_ok, prob_ok = (
            sem(n) for n in ("s_done", "s_bound_ok", "s_max_ok", "exp_ok", "rinv_ok", "prob_ok"))
        pt_done, pt_hi_ok, pt_lo_ok = sem("pt_done"), sem("pt_hi_ok"), sem("pt_lo_ok")
        o_done, ot_hi_ok, ot_lo_ok = sem("o_done"), sem("ot_hi_ok"), sem("ot_lo_ok")
        wo_done, acc_ok = sem("wo_done"), sem("acc_ok")
        gu_hi_ok, gu_lo_ok, dn_hi_ok, dn_lo_ok = (sem(n) for n in ("gu_hi_ok", "gu_lo_ok", "dn_hi_ok", "dn_lo_ok"))
        gate_done, up_done, silu_ok, hid_ok, hid_hi_ok, hid_lo_ok, y_done, y_ok = (
            sem(n) for n in ("gate_done", "up_done", "silu_ok", "hid_ok", "hid_hi_ok", "hid_lo_ok", "y_done", "y_ok"))

        LEAD_Q = HALF + 1
        LEAD_KV = HALF

        def f32(ap):
            return ap.bitcast(F32)

        def c_part(t, b):
            return t[:, b * KC * P:(b + 1) * KC * P]

        def xn_part(t, b):
            return t[:, b // HALF, :, (b % HALF) * P:(b % HALF + 1) * P]

        def chunks(ap):
            return ap.rearrange("p (k r) -> p k r", k=KC)

        def heads(ap):
            return ap.rearrange("p (h r) -> p h r", h=HPG)

        def over_heads(ap):
            return ap.unsqueeze(1).broadcast_to([P, HPG, P])

        def attention_slots(engine, slot):
            with engine.Fori(0, G - 1) as g:
                for b in range(B):
                    slot(g, b, False)
            for b in range(B):
                slot(G - 1, b, True)

        def mlp_steps(engine, step):
            for half in range(2):
                step(0, half, 0)
                with engine.Fori(0, (FC - 3) // 2) as i:
                    for j in (1, 2):
                        step(i, half, j)
                for f in (FC - 2, FC - 1):
                    step(0, half, f)

        def fw_loads(i, t0):
            return (i + (t0 // 2 + 1)) * 16

        block = ctx.enter_context(nc.Block())

        @block.sync
        def _(sp):
            def load_c(b):
                sp.dma_start(q_rot[:, b // HALF, b % HALF, :], ctx_t[b].rearrange("p k r -> p (k r)")).then_inc(c_in[b], 16)

            def load_x(b):
                sp.dma_start(acc[:, b, :], x[b]).then_inc(x_in[b], 16)

            for b in range(HALF):
                load_x(b)
            sp.dma_start(idn[:, :], ident).then_inc(ident_in, 16)
            sp.dma_start(wq_raw[:, :], wq[0]).then_inc(wq_in, 16)
            load_c(0)
            sp.dma_start(wkv_raw[:, :], wkv[0]).then_inc(wkv_in, 16)
            load_x(HALF)
            sp.dma_start(tables[:, :, :], rope.rearrange("n p r -> p n r")).then_inc(tables_in, 16)
            for b in range(1, HALF):
                load_c(b)
                load_x(HALF + b)
            sp.dma_start(bound[:, :, :], mask).then_inc(mask_in, 16)
            for b in range(HALF, B):
                load_c(b)
            sp.dma_start(gate_in[:, :], gates).then_inc(gates_in, 16)
            sp.dma_start(wo_raw[:, :], wo[0]).then_inc(wo_in, 16)
            with sp.Fori(0, G - 1) as g:
                sp.wait_ge(wq_hi_ok, g * HPG + HPG)
                sp.wait_ge(wq_lo_ok, g * HPG + HPG)
                sp.dma_start(wq_raw[:, :], wq[g + 1]).then_inc(wq_in, 16)
                sp.wait_ge(wkv_hi_ok, g + 1)
                sp.wait_ge(wkv_lo_ok, g + 1)
                sp.dma_start(wkv_raw[:, :], wkv[g + 1]).then_inc(wkv_in, 16)
                sp.wait_ge(wo_hi_ok, g * HPG + HPG)
                sp.wait_ge(wo_lo_ok, g * HPG + HPG)
                sp.dma_start(wo_raw[:, :], wo[g + 1]).then_inc(wo_in, 16)

            def load_gu(f, par):
                sp.dma_start(fw_raw[par][:, 0:GU], w_ffn[f][:, 0:GU]).then_inc(gu_in[par], 16)

            def load_dn(f, par):
                sp.dma_start(fw_raw[par][:, GU:FW], w_ffn[f][:, GU:FW]).then_inc(dn_in[par], 16)

            def load_fw(t, f, par):
                sp.wait_ge(gu_hi_ok, t - 1)
                sp.wait_ge(gu_lo_ok, t - 1)
                load_gu(f, par)
                sp.wait_ge(dn_hi_ok, t - 1)
                sp.wait_ge(dn_lo_ok, t - 1)
                load_dn(f, par)

            def store(half):
                for b in range(half * HALF, (half + 1) * HALF):
                    sp.wait_ge(y_ok, b + 1)
                    sp.dma_start(out[b], acc[:, b, :]).then_inc(out_stored, 16)

            sp.wait_ge(wq_hi_ok, G * HPG)
            sp.wait_ge(wq_lo_ok, G * HPG)
            load_gu(0, 0)
            load_dn(0, 0)
            sp.wait_ge(wo_hi_ok, G * HPG)
            sp.wait_ge(wo_lo_ok, G * HPG)
            load_gu(1, 1)
            load_dn(1, 1)
            with sp.Fori(0, (FC - 3) // 2) as i:
                for j in (2, 3):
                    load_fw(i * 2 + j, i * 2 + j, j % 2)
            load_fw(FC - 1, FC - 1, (FC - 1) % 2)
            for f in range(3):
                load_fw(FC + f, f, (FC + f) % 2)
            store(0)
            with sp.Fori(0, (FC - 3) // 2) as i:
                for j in (3, 4):
                    load_fw(i * 2 + (FC + j), i * 2 + j, (FC + j) % 2)
            store(1)
            sp.wait_ge(out_stored, 16 * B)

        @block.tensor
        def _(pe):
            def product(out_ps, lhs, rhs, first=True, last=True):
                (lh, ll), (rh, rl) = lhs, rhs
                pe.matmul(out_ps, lh, rh, start=first, stop=False)
                pe.matmul(out_ps, lh, rl, start=False, stop=False)
                return pe.matmul(out_ps, ll, rh, start=False, stop=last)

            def transpose_xn(b, total):
                pe.wait_ge(ln_rows, total + 1)
                if total < B:
                    if total > 1:
                        pe.wait_ge(xn_lo_ok, total - 1)
                else:
                    pe.wait_ge(xn_lo_ok, total)
                    pe.wait_ge(k_rot_ok, UNITS - B + min(b + 5, B))
                for k in range(KC):
                    mm = pe.transpose(ps_x[total // B][b % 2][:, k * P:(k + 1) * P], xn[:, b % 2, k * P:(k + 1) * P], idn[:, :])
                mm.then_inc(xt_done, 1)

            def project_q(n, head, half, ps, parts):
                for k in parts:
                    mm = product(ps[:, :], (wq_hi[:, head, k, :], wq_lo[:, head, k, :]),
                                 (xn_hi[:, half, k, :], xn_lo[:, half, k, :]), k == 0, k == KC - 1)
                if KC - 1 in parts:
                    mm.then_inc(q_done, 1)

            def project_kv(b):
                for k in range(KC):
                    c = slice((b * KC + k) * P, (b * KC + k + 1) * P)
                    mm = product(ps_kv, (c_hi[:, c], c_lo[:, c]), (wkv_hi[:, k, :], wkv_lo[:, k, :]),
                                 k == 0, k == KC - 1)
                mm.then_inc(kv_done, 1)

            def scores(b):
                for h in range(HPG):
                    q = q_rot[:, b // HALF, h, (b % HALF) * P:(b % HALF + 1) * P]
                    mm = pe.matmul(ps_s[:, h * P:(h + 1) * P], q, k_rot[:, b, :], start=True, stop=True)
                mm.then_inc(s_done, 1)

            def transpose_k(n, first=False):
                pe.wait_ge(k_rows_ok, n + 1)
                if not first:
                    pe.wait_ge(k_rot_ok, n)
                pe.transpose(ps_kt, k_rows[:, :], idn[:, :]).then_inc(kt_done, 1)

            pe.wait_ge(ident_in, 16)
            for b in range(HALF):
                transpose_xn(b, b)
            pe.wait_ge(xn_hi_ok, HALF)
            pe.wait_ge(xn_lo_ok, HALF)
            for n in range(HPG):
                pe.wait_ge(wq_hi_ok, n + 1)
                pe.wait_ge(wq_lo_ok, n + 1)
                if n >= 2:
                    pe.wait_ge(q_cos_ok, n - 1)
                project_q(n, n, 0, ps_q[n % 2], range(KC))
                pe.wait_ge(c_hi_ok, n + 1)
                pe.wait_ge(c_lo_ok, n + 1)
                if n == 0:
                    pe.wait_ge(wkv_hi_ok, 1)
                    pe.wait_ge(wkv_lo_ok, 1)
                else:
                    pe.wait_ge(v_lo_ok, n)
                project_kv(n)
                if n > 0:
                    transpose_k(n - 1, first=n == 1)
                    transpose_xn(HALF + n - 1, HALF + n - 1)
            transpose_xn(B - 1, B - 1)
            pe.wait_ge(q_rot_ok, HPG)
            pe.wait_ge(k_rot_ok, 1)
            scores(0)
            pe.wait_ge(xn_hi_ok, B)
            pe.wait_ge(xn_lo_ok, B)
            pe.wait_ge(q_cos_ok, HPG - 1)
            project_q(HPG, 0, 1, ps_q[HPG % 2], range(KC))
            pe.wait_ge(c_hi_ok, B)
            pe.wait_ge(c_lo_ok, B - 2)
            pe.wait_ge(c_lo_dve_ok, 2)

            def project_out(g, b):
                n = g * B + (b + 1)
                pe.wait_ge(ot_hi_ok, n)
                pe.wait_ge(ot_lo_ok, n)
                for h in range(HPG):
                    if b == 0:
                        pe.wait_ge(wo_hi_ok, g * HPG + (h + 1))
                        pe.wait_ge(wo_lo_ok, g * HPG + (h + 1))
                    c = slice(h * P, (h + 1) * P)
                    mm = product(ps_wo[:, :], (ot_hi[:, c], ot_lo[:, c]), (wo_hi[:, h, :], wo_lo[:, h, :]),
                                 h == 0, h == HPG - 1)
                mm.then_inc(wo_done, 1)

            def gate_or_up(which, ps, done, t, half, par):
                pe.wait_ge(gu_hi_ok, t + 1)
                pe.wait_ge(gu_lo_ok, t + 1)
                for k in range(KC):
                    c = slice((which * KC + k) * P, (which * KC + k + 1) * P)
                    mm = product(ps[:, :], (fw_hi[par][:, c], fw_lo[par][:, c]),
                                 (xn_hi[:, half, k, :], xn_lo[:, half, k, :]), k == 0, k == KC - 1)
                mm.then_inc(done, 1)

            def gate(t, half, par):
                gate_or_up(0, ps_gate[par], gate_done, t, half, par)

            def up(t, half, par):
                gate_or_up(1, ps_up[par], up_done, t, half, par)

            def slot(g, b, last):
                u = g * B
                pe.wait_ge(prob_ok, u + (b + 1))
                for h in range(HPG):
                    mm = pe.transpose(ps_pt[:, h * P:(h + 1) * P], prob[:, b % 2, h, :], idn[:, :])
                mm.then_inc(pt_done, 1)
                if not (last and b == B - 1):
                    nb = (b + 1) % B
                    pe.wait_ge(q_rot_ok, u + (4 * ((b + 1) // 4) + 4))
                    pe.wait_ge(k_rot_ok, u + (b + 2))
                    scores(nb)
                n = b + LEAD_Q
                project = not last or n < B
                if project:
                    if n >= B:
                        pe.wait_ge(wq_hi_ok, g * HPG + (HPG + min(n - B, HPG - 1) + 1))
                        pe.wait_ge(wq_lo_ok, g * HPG + (HPG + min(n - B, HPG - 1) + 1))
                    pe.wait_ge(q_cos_ok, u + (n - 1))
                    where = (n, n % HPG, (n // HPG) % 2, ps_q[n % 2])
                    project_q(*where, range(0, KC // 2))
                if last and b > 0:
                    if b > 1:
                        transpose_xn(b - 2, B + b - 2)
                        pe.wait_ge(acc_ok, u + (b - 1))
                    project_out(g, b - 1)
                pe.wait_ge(pt_hi_ok, u + (b + 1))
                pe.wait_ge(pt_lo_ok, u + (b + 1))
                pe.wait_ge(v_hi_ok, u + (b + 1))
                pe.wait_ge(v_lo_ok, u + (b + 1))
                product(ps_o[:, :], (v_hi[:, b, :], v_lo[:, b, :]), (pt_hi[:, :], pt_lo[:, :])).then_inc(o_done, 1)
                if project:
                    project_q(*where, range(KC // 2, KC))
                if not last or b + 3 < B:
                    if last and b > 1:
                        pe.wait_ge(xn_lo_ok, B + b - 1)
                    transpose_k(u + (b + 3))
                n = b + LEAD_KV
                if not last or n < B:
                    if n >= B:
                        pe.wait_ge(wkv_hi_ok, g + 2)
                        pe.wait_ge(wkv_lo_ok, g + 2)
                    pe.wait_ge(v_lo_ok, u + n)
                    project_kv(n % B)
                if not last:
                    project_out(g, b)
                elif b == B - 2:
                    pe.wait_ge(xn_hi_ok, B + HALF)
                    pe.wait_ge(xn_lo_ok, B + HALF)
                    gate(0, 0, 0)
                elif b == B - 1:
                    up(0, 0, 0)

            attention_slots(pe, slot)
            transpose_xn(B - 2, 2 * B - 2)
            pe.wait_ge(acc_ok, UNITS - 1)
            project_out(G - 1, B - 1)

            def step(i, half, j):
                t0 = half * FC + j
                t, par = i * 2 + t0, t0 % 2
                first, last = j == 0, j == FC - 1
                if not (half == 1 and last):
                    if last:
                        pe.wait_ge(xn_hi_ok, 2 * B)
                        pe.wait_ge(xn_lo_ok, 2 * B)
                    if t0 > 0:
                        pe.wait_ge(silu_ok, t)
                        pe.wait_ge(hid_ok, t)
                    gate(t + 1, 1 if last else half, 1 - par)
                    up(t + 1, 1 if last else half, 1 - par)
                    if t0 == 0:
                        transpose_xn(B - 1, 2 * B - 1)
                pe.wait_ge(hid_hi_ok, t + 1)
                pe.wait_ge(hid_lo_ok, t + 1)
                pe.wait_ge(dn_hi_ok, t + 1)
                pe.wait_ge(dn_lo_ok, t + 1)
                if t0 == 0:
                    pe.wait_ge(xn_lo_ok, 2 * B)
                elif first:
                    pe.wait_ge(y_ok, HALF)
                for r in range(HALF):
                    c = slice(r * P, (r + 1) * P)
                    mm = product(ps_y[r][:, :], (hid_hi[par][:, c], hid_lo[par][:, c]),
                                 (fw_hi[par][:, GU:FW], fw_lo[par][:, GU:FW]), first, last)
                    if last:
                        mm.then_inc(y_done, 1)

            mlp_steps(pe, step)

        @block.scalar
        def _(act):
            def split_c(b):
                act.wait_ge(c_in[b], 16)
                act.activation(c_part(c_hi, b), q_rot[:, b // HALF, b % HALF, :], ACT.Copy).then_inc(c_hi_ok, 1)

            def split_wq(h, g16):
                act.wait_ge(wq_in, g16)
                act.activation(wq_hi[:, h, :, :].rearrange("p k r -> p (k r)"),
                               wq_raw[:, h * KC * P:(h + 1) * KC * P], ACT.Copy).then_inc(wq_hi_ok, 1)

            def split_wkv(g16):
                act.wait_ge(wkv_in, g16)
                act.activation(wkv_hi[:, :, :].rearrange("p k r -> p (k r)"), wkv_raw[:, :], ACT.Copy).then_inc(wkv_hi_ok, 1)

            def split_xn(b, total):
                act.wait_ge(xt_done, total + 1)
                act.activation(xn_part(xn_hi, b), chunks(ps_x[total // B][b % 2][:, :]), ACT.Copy).then_inc(xn_hi_ok, 1)

            def swap_q(ps, nq):
                act.wait_ge(q_done, nq + 1)
                act.wait_ge(q_sin_ok, nq)
                act.activation(q_swap[0:P // 2, :], ps[P // 2:P, :], ACT.Copy)
                act.activation(q_swap[P // 2:P, :], ps[0:P // 2, :], ACT.Copy).then_inc(q_swap_ok, 1)

            def take_v(b, n):
                act.wait_ge(kv_done, n + 1)
                act.activation(v_hi[:, b, :], ps_kv[:, P:2 * P], ACT.Copy).then_inc(v_hi_ok, 1)

            def take_kt(b, n):
                act.wait_ge(kt_done, n + 1)
                act.activation(k_rot[:, b, :], ps_kt, ACT.Copy).then_inc(k_rot_ok, 1)

            def exponentials(par, n):
                act.wait_ge(s_max_ok, n + 1)
                for h in range(HPG):
                    e = act.activation(prob[:, par, h, :], ps_s[:, h * P:(h + 1) * P], ACT.Exp,
                                       bias=nmax[:, par, h:h + 1], scale=-1.0, accum_out=rsum[:, par, h:h + 1])
                e.then_inc(exp_ok, 1)

            for b in range(HALF):
                split_xn(b, b)
            for h in range(HPG):
                split_wq(h, 16)
            split_c(0)
            split_wkv(16)
            for n in range(HPG):
                swap_q(ps_q[n % 2], n)
                take_v(n, n)
                if n > 0:
                    take_kt(n - 1, n - 1)
                    split_xn(HALF + n - 1, HALF + n - 1)
                if n + 1 < HALF:
                    split_c(n + 1)
                else:
                    split_xn(B - 1, B - 1)
                if n >= 2:
                    split_c(HALF + n - 2)
            split_c(B - 2)
            split_c(B - 1)
            act.wait_ge(gates_in, 16)
            act.activation(gate_tanh[:, :], gate_in[:, :], ACT.Tanh).then_inc(tanh_ok, 1)
            exponentials(0, 0)
            swap_q(ps_q[HPG % 2], HPG)

            def split_gu(par, loaded):
                act.wait_ge(gu_in[par], loaded)
                act.activation(fw_hi[par][:, 0:GU], fw_raw[par][:, 0:GU], ACT.Copy).then_inc(gu_hi_ok, 1)

            def slot(g, b, last):
                u = g * B
                act.wait_ge(pt_done, u + (b + 1))
                act.activation(pt_hi[:, :], ps_pt[:, :], ACT.Copy).then_inc(pt_hi_ok, 1)
                if b == 0:
                    act.wait_ge(wo_in, g * 16 + 16)
                    for h in range(HPG):
                        act.activation(wo_hi[:, h, :], wo_raw[:, h * DM:(h + 1) * DM], ACT.Copy).then_inc(wo_hi_ok, 1)
                if last:
                    if b > 1:
                        split_xn(b - 2, B + b - 2)
                    if b < B - 1:
                        exponentials((b + 1) % 2, u + (b + 1))
                act.wait_ge(o_done, u + (b + 1))
                act.activation(ot_hi[:, :], ps_o[:, :], ACT.Copy).then_inc(ot_hi_ok, 1)
                if not last:
                    exponentials((b + 1) % 2, u + (b + 1))
                n = b + LEAD_Q
                if not last or n < B:
                    swap_q(ps_q[n % 2], u + n)
                if not last or b + 3 < B:
                    take_kt((b + 3) % B, u + (b + 3))
                n = b + LEAD_KV
                if not last or n < B:
                    take_v(n % B, u + n)
                if not last:
                    if 1 <= b <= HPG:
                        split_wq(b - 1, g * 16 + 32)
                    if b == HALF - 1:
                        split_wkv(g * 16 + 32)
                elif b in (HALF, HALF + 1):
                    split_gu(b - HALF, 16)

            attention_slots(act, slot)
            split_xn(B - 2, 2 * B - 2)

            def step(i, half, j):
                t0 = half * FC + j
                t, par = i * 2 + t0, t0 % 2
                act.wait_ge(gate_done, t + 1)
                act.activation(silu[par][:, :], ps_gate[par][:, :], ACT.Silu).then_inc(silu_ok, 1)
                act.wait_ge(dn_in[par], fw_loads(i, t0))
                act.activation(fw_hi[par][:, GU:FW], fw_raw[par][:, GU:FW], ACT.Copy).then_inc(dn_hi_ok, 1)
                act.wait_ge(hid_ok, t + 1)
                act.activation(hid_hi[par][:, :], hid[par], ACT.Copy).then_inc(hid_hi_ok, 1)
                if t0 == 0:
                    split_xn(B - 1, 2 * B - 1)
                if t0 < 2 * FC - 2:
                    split_gu(par, fw_loads(i, t0 + 2))

            mlp_steps(act, step)

        @block.vector
        def _(dve):
            def sub(out_lo, whole, hi):
                return dve.tensor_tensor(out_lo, whole, f32(hi), ALU.subtract)

            def ln_stat(b, total):
                dve.bn_stats(stats[:, b, :], acc[:, b, :]).then_inc(ln_stats, 1)
                dve.wait_ge(ln_stats, total + 1)
                dve.bn_aggr(meanvar[:, b, :], stats[:, b, :]).then_inc(ln_aggr, 1)
                dve.wait_ge(ln_aggr, total + 1)
                dve.tensor_scalar(vareps[:, b:b + 1], meanvar[:, b, 1:2], LN_EPS, None, ALU.add).then_inc(ln_var, 1)

            def ln_row(b, total):
                dve.wait_ge(ln_rstd, total + 1)
                if total > 1:
                    dve.wait_ge(xt_done, total - 1)
                dve.tensor_scalar(xn[:, b % 2, :], acc[:, b, :], meanvar[:, b, 0:1], rstd[:, b:b + 1],
                                  ALU.subtract, ALU.mult).then_inc(ln_rows, 1)

            def split_xn(b, total):
                dve.wait_ge(xn_hi_ok, total + 1)
                sub(xn_part(xn_lo, b), chunks(ps_x[total // B][b % 2][:, :]), xn_part(xn_hi, b)).then_inc(xn_lo_ok, 1)

            def rope_k(n):
                dve.wait_ge(v_hi_ok, n + 1)
                dve.tensor_tensor(k_c[:, :], ps_kv[:, 0:P], cos_k, ALU.mult).then_inc(k_cos_ok, 1)
                lo, up = slice(0, P // 2), slice(P // 2, P)
                dve.tensor_tensor(k_s[:, lo], ps_kv[:, up], sin_k[:, lo], ALU.mult)
                dve.tensor_tensor(k_s[:, up], ps_kv[:, lo], sin_k[:, up], ALU.mult).then_inc(k_sin_ok, 1)
                dve.wait_ge(k_cos_ok, n + 1)
                dve.wait_ge(k_sin_ok, n + 1)
                dve.wait_ge(kt_done, n)
                dve.tensor_tensor(k_rows[:, :], k_c[:, :], k_s[:, :], ALU.add).then_inc(k_rows_ok, 1)

            def split_v(b, n):
                sub(v_lo[:, b, :], ps_kv[:, P:2 * P], v_hi[:, b, :]).then_inc(v_lo_ok, 1)

            def split_wkv(count):
                dve.wait_ge(wkv_hi_ok, count)
                sub(wkv_lo[:, :, :].rearrange("p k r -> p (k r)"), wkv_raw[:, :],
                    wkv_hi[:, :, :].rearrange("p k r -> p (k r)")).then_inc(wkv_lo_ok, 1)

            def rope_q(ps, n):
                dve.wait_ge(q_swap_ok, n + 1)
                dve.wait_ge(q_rot_ok, n)
                dve.tensor_tensor(heads(q_c[:, :]), heads(ps[:, :]), over_heads(cos_q), ALU.mult).then_inc(q_cos_ok, 1)
                dve.tensor_tensor(heads(q_s[:, :]), heads(q_swap[:, :]), over_heads(sin_q), ALU.mult).then_inc(q_sin_ok, 1)

            def row_max(b, par, n):
                dve.wait_ge(s_done, n + 1)
                dve.tensor_tensor(heads(ps_s[:, :]), heads(ps_s[:, :]), over_heads(bound[:, b, :]),
                                  ALU.max).then_inc(s_bound_ok, 1)
                dve.wait_ge(s_bound_ok, n + 1)
                dve.tensor_reduce(nmax[:, par, :], heads(ps_s[:, :]), AX_X, ALU.min).then_inc(s_max_ok, 1)

            def invert_sums(par, n):
                dve.wait_ge(exp_ok, n + 1)
                dve.reciprocal(rinv[:, par, :], rsum[:, par, :]).then_inc(rinv_ok, 1)

            def split_c(b):
                dve.wait_ge(c_hi_ok, b + 1)
                sub(c_part(c_lo, b), q_rot[:, b // HALF, b % HALF, :], c_part(c_hi, b)).then_inc(c_lo_dve_ok, 1)

            def ln_first(b):
                dve.wait_ge(x_in[b], 16)
                ln_stat(b, b)

            ln_first(0)
            for b in range(1, HALF):
                ln_first(b)
                ln_row(b - 1, b - 1)
                if b > 1:
                    split_xn(b - 2, b - 2)
            ln_row(HALF - 1, HALF - 1)
            split_xn(HALF - 2, HALF - 2)
            split_xn(HALF - 1, HALF - 1)
            ln_first(HALF)
            split_wkv(1)
            ln_row(HALF, HALF)
            dve.wait_ge(tables_in, 16)
            for n in range(HPG):
                rope_q(ps_q[n % 2], n)
                rope_k(n)
                split_v(n, n)
                if n > 0:
                    split_xn(HALF + n - 1, HALF + n - 1)
                if HALF + n + 1 < B:
                    ln_first(HALF + n + 1)
                    ln_row(HALF + n + 1, HALF + n + 1)
                if n == 2:
                    dve.wait_ge(mask_in, 16)
                    dve.tensor_scalar(bound[:, :, :], bound[:, :, :], 0.0, None, ALU.not_equal).then_inc(bound_cmp, 1)
                    dve.wait_ge(bound_cmp, 1)
                    dve.tensor_scalar(bound[:, :, :], bound[:, :, :], -NO_BOUND, -MASKED, ALU.mult, ALU.add).then_inc(bound_ok, 1)
            split_xn(B - 1, B - 1)
            dve.wait_ge(bound_ok, 1)
            row_max(0, 0, 0)
            split_c(HALF)
            split_c(HALF + 1)
            invert_sums(0, 0)
            rope_q(ps_q[HPG % 2], HPG)
            dve.wait_ge(tanh_ok, 1)

            def add_out(b, n):
                dve.wait_ge(wo_done, n + 1)
                dve.scalar_tensor_tensor(out=acc[:, b, :], in0=ps_wo[:, :], scalar=gate_tanh[:, 0:1],
                                         in1=acc[:, b, :], op0=ALU.mult, op1=ALU.add).then_inc(acc_ok, 1)

            def slot(g, b, last):
                u = g * B
                dve.wait_ge(pt_hi_ok, u + (b + 1))
                sub(pt_lo[:, :], ps_pt[:, :], pt_hi[:, :]).then_inc(pt_lo_ok, 1)
                more = not (last and b == B - 1)
                if more:
                    row_max((b + 1) % B, (b + 1) % 2, u + (b + 1))
                if last and b > 0:
                    if b > 1:
                        split_xn(b - 2, B + b - 2)
                    add_out(b - 1, u + (b - 1))
                    if more:
                        invert_sums((b + 1) % 2, u + (b + 1))
                dve.wait_ge(ot_hi_ok, u + (b + 1))
                sub(ot_lo[:, :], ps_o[:, :], ot_hi[:, :]).then_inc(ot_lo_ok, 1)
                if last and b > 0:
                    dve.wait_ge(acc_ok, u + b)
                    ln_stat(b - 1, B + b - 1)
                    ln_row(b - 1, B + b - 1)
                else:
                    invert_sums((b + 1) % 2, u + (b + 1))
                n = b + LEAD_Q
                if not last or n < B:
                    rope_q(ps_q[n % 2], u + n)
                n = b + LEAD_KV
                if not last or n < B:
                    rope_k(u + n)
                    split_v(n % B, u + n)
                if not last and b == HALF - 1:
                    split_wkv(g + 2)
                if not last:
                    add_out(b, u + b)

            attention_slots(dve, slot)
            split_xn(B - 2, 2 * B - 2)
            add_out(B - 1, UNITS - 1)
            dve.wait_ge(acc_ok, UNITS)
            ln_stat(B - 1, 2 * B - 1)
            ln_row(B - 1, 2 * B - 1)

            def step(i, half, j):
                t0 = half * FC + j
                t, par = i * 2 + t0, t0 % 2
                dve.wait_ge(silu_ok, t + 1)
                dve.wait_ge(up_done, t + 1)
                dve.tensor_tensor(hid[par], ps_up[par][:, :], silu[par][:, :], ALU.mult).then_inc(hid_ok, 1)
                dve.wait_ge(hid_hi_ok, t + 1)
                sub(hid_lo[par][:, :], hid[par], hid_hi[par][:, :]).then_inc(hid_lo_ok, 1)
                if t0 == 0:
                    split_xn(B - 1, 2 * B - 1)
                if j == FC - 1:
                    for r in range(HALF):
                        b = half * HALF + r
                        dve.wait_ge(y_done, b + 1)
                        dve.scalar_tensor_tensor(out=acc[:, b, :], in0=ps_y[r][:, :], scalar=gate_tanh[:, 1:2],
                                                 in1=acc[:, b, :], op0=ALU.mult, op1=ALU.add).then_inc(y_ok, 1)

            mlp_steps(dve, step)

        @block.gpsimd
        def _(pool):
            def sub(out_lo, whole, hi):
                return pool.tensor_tensor(out_lo, whole, f32(hi), ALU.subtract)

            def split_c(b):
                pool.wait_ge(c_hi_ok, b + 1)
                sub(c_part(c_lo, b), q_rot[:, b // HALF, b % HALF, :], c_part(c_hi, b)).then_inc(c_lo_ok, 1)

            def ln_power(b, total):
                pool.wait_ge(ln_var, total + 1)
                pool.tensor_tensor(rstd[:, b:b + 1], vareps[:, b:b + 1], minus_half[:, b:b + 1],
                                   ALU.pow).then_inc(ln_rstd, 1)

            def split_wq(h, count):
                pool.wait_ge(wq_hi_ok, count)
                sub(wq_lo[:, h, :, :].rearrange("p k r -> p (k r)"), wq_raw[:, h * KC * P:(h + 1) * KC * P],
                    wq_hi[:, h, :, :].rearrange("p k r -> p (k r)")).then_inc(wq_lo_ok, 1)

            def add_q(half, head, n):
                pool.wait_ge(q_cos_ok, n + 1)
                pool.wait_ge(q_sin_ok, n + 1)
                pool.tensor_tensor(q_rot[:, half, head, :], q_c[:, :], q_s[:, :], ALU.add).then_inc(q_rot_ok, 1)

            def normalise(par, n):
                pool.wait_ge(rinv_ok, n + 1)
                p4 = prob[:, par, :, :]
                pool.tensor_tensor(p4, p4, rinv[:, par, :].unsqueeze(2).broadcast_to([P, HPG, P]),
                                   ALU.mult).then_inc(prob_ok, 1)

            pool.memset(minus_half[:, :], -0.5).then_inc(half_ok, 1)
            pool.wait_ge(half_ok, 1)
            for b in range(HALF):
                ln_power(b, b)
            split_wq(0, 1)
            ln_power(HALF, HALF)
            for h in range(1, HPG):
                split_wq(h, h + 1)
            split_c(0)
            for n in range(HPG):
                pool.wait_ge(c_lo_ok, n + 1)
                add_q(0, n, n)
                if n + 1 < HALF:
                    ln_power(HALF + n + 1, HALF + n + 1)
                    split_c(n + 1)
            split_c(B - 2)
            split_c(B - 1)
            normalise(0, 0)
            pool.wait_ge(c_lo_ok, B - 2)
            pool.wait_ge(c_lo_dve_ok, 2)
            add_q(1, 0, HPG)

            def split_gu(t, par):
                pool.wait_ge(gu_hi_ok, t + 1)
                sub(fw_lo[par][:, 0:GU], fw_raw[par][:, 0:GU], fw_hi[par][:, 0:GU]).then_inc(gu_lo_ok, 1)

            def slot(g, b, last):
                u = g * B
                if b == 0:
                    for h in range(HPG):
                        pool.wait_ge(wo_hi_ok, g * HPG + (h + 1))
                        sub(wo_lo[:, h, :], wo_raw[:, h * DM:(h + 1) * DM], wo_hi[:, h, :]).then_inc(wo_lo_ok, 1)
                if not (last and b == B - 1):
                    normalise((b + 1) % 2, u + (b + 1))
                if last and b > 0:
                    ln_power(b - 1, B + b - 1)
                n = b + LEAD_Q
                if not last or n < B:
                    add_q((n // HPG) % 2, n % HPG, u + n)
                if not last and 1 <= b <= HPG:
                    split_wq(b - 1, g * HPG + (HPG + b))
                if last and b in (HALF, HALF + 1):
                    split_gu(b - HALF, b - HALF)

            attention_slots(pool, slot)
            ln_power(B - 1, 2 * B - 1)

            def step(i, half, j):
                t0 = half * FC + j
                t, par = i * 2 + t0, t0 % 2
                pool.wait_ge(dn_hi_ok, t + 1)
                sub(fw_lo[par][:, GU:FW], fw_raw[par][:, GU:FW], fw_hi[par][:, GU:FW]).then_inc(dn_lo_ok, 1)
                if t0 < 2 * FC - 2:
                    split_gu(t + 2, par)

            mlp_steps(pool, step)


def rope_tables(n_rows, dim, np):
    inv_freq = 1.0 / np.float32(10000.0) ** (np.arange(0, dim, 2, dtype=np.float32) / np.float32(dim))
    ang = np.arange(n_rows, dtype=np.float32)[:, None] * inv_freq[None, :].astype(np.float32)
    cos, sin = np.cos(ang), np.sin(ang)
    cos = np.concatenate([cos, cos], axis=1)
    sin = np.concatenate([-sin, sin], axis=1)
    by = -1.0 / np.sqrt(np.float64(dim))
    return np.stack([cos.T * by, sin.T * by, cos, sin]).astype(np.float32)


def kernel(x, ctx_4096, mask_BxSxS2_ff1, g_xattn, g_ffn, L0_xattn_wq, L0_xattn_wk, L0_xattn_wv, L0_xattn_wo,
           L0_ffn_W_gate, L0_ffn_W_up, L0_ffn_W_down):
    import numpy as np
    import concourse.bacc as bacc
    from concourse.bass_utils import run_bass_kernel_spmd

    x, c, mask, g_x, g_f, wq, wk, wv, wo, w_gate, w_up, w_down = (
        np.asarray(a) for a in (x, ctx_4096, mask_BxSxS2_ff1, g_xattn, g_ffn, L0_xattn_wq, L0_xattn_wk,
                                L0_xattn_wv, L0_xattn_wo, L0_ffn_W_gate, L0_ffn_W_up, L0_ffn_W_down))
    B, S, DM = x.shape
    KC, G = DM // P, wk.shape[1] // P
    HPG = wq.shape[1] // (G * P)
    F = w_gate.shape[0]
    FC = -(-F // P)
    pad = FC * P - F

    def kcols(w, heads):
        return w.reshape(KC, P, G, heads, P).transpose(2, 1, 3, 0, 4)

    def chunked(w):
        return np.pad(w, ((0, pad), (0, 0))).reshape(FC, P, KC, P).transpose(0, 3, 2, 1)

    wkv = np.concatenate([kcols(wk, 1)[:, :, 0], kcols(wv, 1)[:, :, 0]], axis=3)
    down = np.pad(w_down.T, ((0, pad), (0, 0))).reshape(FC, P, DM)
    w_ffn = np.concatenate([chunked(w_gate).reshape(FC, P, KC * P), chunked(w_up).reshape(FC, P, KC * P), down], axis=2)
    gates = np.empty((P, 2), x.dtype)
    gates[:, 0], gates[:, 1] = g_x[0], g_f[0]
    arrays = {
        "x": x,
        "ctx_t": c.reshape(B, S, KC, P).transpose(0, 3, 2, 1),
        "mask": mask.transpose(1, 0, 2),
        "gates": gates,
        "wq": kcols(wq, HPG).reshape(G, P, HPG * KC * P),
        "wkv": wkv.reshape(G, P, KC * 2 * P),
        "wo": wo.reshape(G, HPG, P, DM).transpose(0, 2, 1, 3).reshape(G, P, HPG * DM),
        "w_ffn": w_ffn,
        "rope": rope_tables(S, P, np),
        "ident": np.eye(P, dtype=np.float32),
    }
    arrays = {f"in_{n}": np.ascontiguousarray(a) for n, a in arrays.items()}
    nc = bacc.Bacc("TRN2", target_bir_lowering=False, num_devices=1)
    ins = [nc.dram_tensor(n, a.shape, mybir.dt.from_np(a.dtype), kind="ExternalInput").ap() for n, a in arrays.items()]
    out = nc.dram_tensor("out_0", (B, S, DM), F32, kind="ExternalOutput").ap()
    gated_cross_attention_block(nc, *ins, out)
    r = run_bass_kernel_spmd(nc, [arrays], core_ids=[0])
    return r.results[0]["out_0"]
```

```python
from contextlib import ExitStack

import concourse.bass as bass
from concourse import mybir

P = 128
F32 = mybir.dt.float32
F32R = mybir.dt.float32r
ALU = mybir.AluOpType
ACT = mybir.ActivationFunctionType
AX_X = mybir.AxisListType.X
LN_EPS = 1e-5
MASKED = -1e9
NO_BOUND = 3e38
WARM = [6, 2, 2]


def gated_cross_attention_block(
    nc: bass.Bass,
    x: bass.AP,
    ctx_t: bass.AP,
    mask: bass.AP,
    gates: bass.AP,
    wq: bass.AP,
    wkv: bass.AP,
    wo: bass.AP,
    w_ffn: bass.AP,
    rope: bass.AP,
    ident: bass.AP,
    out: bass.AP,
):
    B, S, DM = x.shape
    KC = DM // P
    G = wq.shape[0]
    HPG = wo.shape[2] // DM
    FC = w_ffn.shape[0]
    HALF = B // 2
    ROWS = HALF * S
    UNITS = G * B
    GU = KC * 2 * P
    assert S == P and ROWS == 512 and DM == 512 and HPG * P == 512 and B == 8 and FC % 2 == 1

    with ExitStack() as ctx:
        def sb(name, shape, dt=F32):
            return ctx.enter_context(nc.sbuf_tensor(name, shape, dt))

        def sem(name):
            return ctx.enter_context(nc.semaphore(name))

        xn_hi = sb("xn_hi", [P, 2, KC, ROWS], F32R)
        xn_lo = sb("xn_lo", [P, 2, KC, ROWS], F32R)
        c_hi = sb("c_hi", [P, B * KC * P], F32R)
        c_lo = sb("c_lo", [P, B * KC * P], F32R)
        wq_hi = sb("wq_hi", [P, HPG, KC, P], F32R)
        wq_lo = sb("wq_lo", [P, HPG, KC, P], F32R)
        wkv_hi = sb("wkv_hi", [P, KC, 2 * P], F32R)
        wkv_lo = sb("wkv_lo", [P, KC, 2 * P], F32R)
        wo_hi = sb("wo_hi", [P, HPG, DM], F32R)
        wo_lo = sb("wo_lo", [P, HPG, DM], F32R)
        v_hi = sb("v_hi", [P, B, P], F32R)
        v_lo = sb("v_lo", [P, B, P], F32R)
        pt_hi = sb("pt_hi", [P, HPG * P], F32R)
        pt_lo = sb("pt_lo", [P, HPG * P], F32R)
        ot_hi = sb("ot_hi", [P, HPG * P], F32R)
        ot_lo = sb("ot_lo", [P, HPG * P], F32R)

        acc = sb("acc", [P, B, DM])
        wq_raw = sb("wq_raw", [P, HPG * KC * P])
        wkv_raw = sb("wkv_raw", [P, KC * 2 * P])
        wo_raw = sb("wo_raw", [P, HPG * DM])
        q_rot = sb("q_rot", [P, 2, HPG, ROWS])
        k_rot = sb("k_rot", [P, B, P])
        k_rows = sb("k_rows", [P, P])
        bound = sb("bound", [P, B, S])
        tables = sb("tables", [P, 4, P])
        cos_q, sin_q, cos_k, sin_k = (tables[:, n, :] for n in range(4))
        idn = sb("idn", [P, P])
        q_swap = sb("q_swap", [P, ROWS])
        q_c = sb("q_c", [P, ROWS])
        q_s = sb("q_s", [P, ROWS])
        k_c = sb("k_c", [P, P])
        k_s = sb("k_s", [P, P])
        prob = sb("prob", [P, 2, HPG, P])
        xn = sb("xn", [P, 2, DM])
        nmax = sb("nmax", [P, 2, HPG])
        rsum = sb("rsum", [P, 2, HPG])
        rinv = sb("rinv", [P, 2, HPG])
        stats = sb("stats", [P, B, 6])
        meanvar = sb("meanvar", [P, B, 2])
        vareps = sb("vareps", [P, B])
        rstd = sb("rstd", [P, B])
        minus_mean = sb("minus_mean", [P, B])
        minus_half = sb("minus_half", [P, B])
        gate_in = sb("gate_in", [P, 2])
        gate_tanh = sb("gate_tanh", [P, 2])

        bank = [ctx.enter_context(nc.psum_tensor(f"bank{n}", [P, 512], F32)) for n in range(8)]
        ps_q = [bank[0], bank[1]]
        ps_kv = bank[2][:, 0:2 * P]
        ps_s, ps_pt, ps_o, ps_wo = bank[3], bank[4], bank[5], bank[6]
        ps_kv2 = ps_pt[:, 0:2 * P]
        ps_kt = bank[7][:, 0:P]
        ps_x = [[bank[6], bank[5]] * HALF, [bank[7], bank[7]] + [bank[2], bank[7]] * (HALF - 1)]
        ps_gate = [bank[0], bank[4]]
        ps_up = [bank[1], bank[5]]
        ps_y = [bank[2], bank[3], bank[6], bank[7]]

        fw_raw = [wq_raw, wo_raw]
        FW = GU + DM
        fw_hi = [c_hi[:, n * FW:(n + 1) * FW] for n in range(2)]
        fw_lo = [c_lo[:, n * FW:(n + 1) * FW] for n in range(2)]
        silu = [q_c, q_s]
        hid = [prob[:, n, :, :].rearrange("p h k -> p (h k)") for n in range(2)]
        hid_hi = [pt_hi, ot_hi]
        hid_lo = [pt_lo, ot_lo]

        ident_in, tables_in = sem("ident_in"), sem("tables_in")
        x_in = [sem(f"x_in{b}") for b in range(B)]
        c_in = [sem(f"c_in{b}") for b in range(B)]
        mask_in, gates_in = sem("mask_in"), sem("gates_in")
        wq_first_in = sem("wq_first_in")
        wq_in, wkv_in, wo_in = sem("wq_in"), sem("wkv_in"), sem("wo_in")
        gu_in = [sem("gu_in0"), sem("gu_in1")]
        dn_in = [sem("dn_in0"), sem("dn_in1")]
        out_stored = sem("out_stored")
        c_hi_ok, c_lo_ok, c_lo_dve_ok = sem("c_hi_ok"), sem("c_lo_ok"), sem("c_lo_dve_ok")
        wq_hi_ok, wq_lo_ok = sem("wq_hi_ok"), sem("wq_lo_ok")
        wkv_hi_ok, wkv_lo_ok = sem("wkv_hi_ok"), sem("wkv_lo_ok")
        wo_hi_ok, wo_lo_ok = sem("wo_hi_ok"), sem("wo_lo_ok")
        ln_var4, ln_rstd4 = sem("ln_var4"), sem("ln_rstd4")
        ln_stats, ln_aggr, ln_var, ln_rstd, ln_rows = (sem(n) for n in ("ln_stats", "ln_aggr", "ln_var", "ln_rstd", "ln_rows"))
        half_ok = sem("half_ok")
        ln_mean, ln_centred = sem("ln_mean"), sem("ln_centred")
        xt_done, xn_hi_ok, xn_lo_ok = sem("xt_done"), sem("xn_hi_ok"), sem("xn_lo_ok")
        bound_cmp, bound_ok, tanh_ok = sem("bound_cmp"), sem("bound_ok"), sem("tanh_ok")
        q_done, q_swap_ok, q_cos_ok, q_sin_ok, q_rot_ok = (
            sem(n) for n in ("q_done", "q_swap_ok", "q_cos_ok", "q_sin_ok", "q_rot_ok"))
        kv_done, k_cos_ok, k_sin_ok, k_rows_ok, kt_done, k_rot_ok = (
            sem(n) for n in ("kv_done", "k_cos_ok", "k_sin_ok", "k_rows_ok", "kt_done", "k_rot_ok"))
        v_hi_ok, v_lo_ok = sem("v_hi_ok"), sem("v_lo_ok")
        s_done, s_bound_ok, s_max_ok, exp_ok, rinv_ok, prob_ok = (
            sem(n) for n in ("s_done", "s_bound_ok", "s_max_ok", "exp_ok", "rinv_ok", "prob_ok"))
        pt_done, pt_hi_ok, pt_lo_ok = sem("pt_done"), sem("pt_hi_ok"), sem("pt_lo_ok")
        o_done, ot_hi_ok, ot_lo_ok = sem("o_done"), sem("ot_hi_ok"), sem("ot_lo_ok")
        wo_done, acc_ok = sem("wo_done"), sem("acc_ok")
        gu_hi_ok, gu_lo_ok, dn_hi_ok, dn_lo_ok = (sem(n) for n in ("gu_hi_ok", "gu_lo_ok", "dn_hi_ok", "dn_lo_ok"))
        gate_done, up_done, silu_ok, hid_ok, hid_hi_ok, hid_lo_ok, y_done, y_ok = (
            sem(n) for n in ("gate_done", "up_done", "silu_ok", "hid_ok", "hid_hi_ok", "hid_lo_ok", "y_done", "y_ok"))

        LEAD_Q = HALF + 1
        LEAD_KV = HALF

        def f32(ap):
            return ap.bitcast(F32)

        def c_part(t, b):
            return t[:, b * KC * P:(b + 1) * KC * P]

        def xn_part(t, b):
            return t[:, b // HALF, :, (b % HALF) * P:(b % HALF + 1) * P]

        def chunks(ap):
            return ap.rearrange("p (k r) -> p k r", k=KC)

        def heads(ap):
            return ap.rearrange("p (h r) -> p h r", h=HPG)

        def over_heads(ap):
            return ap.unsqueeze(1).broadcast_to([P, HPG, P])

        def attention_slots(engine, slot, closing):
            with engine.Fori(0, G - 1) as g:
                for b in range(B):
                    slot(g, b, False)
            for b in range(2):
                slot(G - 1, b, True)
            for b in range(2, B):
                closing(b)

        def mlp_steps(engine, step):
            for half in range(2):
                step(0, half, 0)
                with engine.Fori(0, (FC - 3) // 2) as i:
                    for j in (1, 2):
                        step(i, half, j)
                for f in (FC - 2, FC - 1):
                    step(0, half, f)

        def fw_loads(i, t0):
            return (i + (t0 // 2 + 1)) * 16

        block = ctx.enter_context(nc.Block())

        @block.sync
        def _(sp):
            def load_c(b):
                sp.dma_start(q_rot[:, b // HALF, b % HALF, :], ctx_t[b].rearrange("p k r -> p (k r)")).then_inc(c_in[b], 16)

            def load_x(b):
                sp.dma_start(acc[:, b, :], x[b]).then_inc(x_in[b], 16)

            load_x(0)
            sp.dma_start(idn[:, :], ident).then_inc(ident_in, 16)
            load_x(1)
            load_x(2)
            sp.dma_start(wq_raw[:, 0:KC * P], wq[0][:, 0:KC * P]).then_inc(wq_first_in, 16)
            load_x(3)
            sp.dma_start(wq_raw[:, KC * P:], wq[0][:, KC * P:]).then_inc(wq_in, 16)
            load_c(0)
            load_x(HALF)
            sp.dma_start(wkv_raw[:, :], wkv[0]).then_inc(wkv_in, 16)
            for b in range(HALF + 1, B):
                load_x(b)
            sp.dma_start(tables[:, :, :], rope.rearrange("n p r -> p n r")).then_inc(tables_in, 16)
            for b in range(1, HALF):
                load_c(b)
            sp.dma_start(bound[:, :, :], mask).then_inc(mask_in, 16)
            for b in range(HALF, B):
                load_c(b)
            sp.dma_start(gate_in[:, :], gates).then_inc(gates_in, 16)
            sp.dma_start(wo_raw[:, :], wo[0]).then_inc(wo_in, 16)
            with sp.Fori(0, G - 1) as g:
                sp.wait_ge(wq_hi_ok, g * HPG + HPG)
                sp.wait_ge(wq_lo_ok, g * HPG + HPG)
                sp.dma_start(wq_raw[:, :], wq[g + 1]).then_inc(wq_in, 16)
                sp.wait_ge(wkv_hi_ok, g + 1)
                sp.wait_ge(wkv_lo_ok, g + 1)
                sp.dma_start(wkv_raw[:, :], wkv[g + 1]).then_inc(wkv_in, 16)
                sp.wait_ge(wo_hi_ok, g * HPG + HPG)
                sp.wait_ge(wo_lo_ok, g * HPG + HPG)
                sp.dma_start(wo_raw[:, :], wo[g + 1]).then_inc(wo_in, 16)

            def load_gu(f, par):
                sp.dma_start(fw_raw[par][:, 0:GU], w_ffn[f][:, 0:GU]).then_inc(gu_in[par], 16)

            def load_dn(f, par):
                sp.dma_start(fw_raw[par][:, GU:FW], w_ffn[f][:, GU:FW]).then_inc(dn_in[par], 16)

            def load_fw(t, f, par):
                sp.wait_ge(gu_hi_ok, t - 1)
                sp.wait_ge(gu_lo_ok, t - 1)
                load_gu(f, par)
                sp.wait_ge(dn_hi_ok, t - 1)
                sp.wait_ge(dn_lo_ok, t - 1)
                load_dn(f, par)

            def store(half):
                for b in range(half * HALF, (half + 1) * HALF):
                    sp.wait_ge(y_ok, b + 1)
                    sp.dma_start(out[b], acc[:, b, :]).then_inc(out_stored, 16)

            sp.wait_ge(wq_hi_ok, G * HPG)
            sp.wait_ge(wq_lo_ok, G * HPG)
            load_gu(0, 0)
            load_dn(0, 0)
            sp.wait_ge(wo_hi_ok, G * HPG)
            sp.wait_ge(wo_lo_ok, G * HPG)
            load_gu(1, 1)
            load_dn(1, 1)
            with sp.Fori(0, (FC - 3) // 2) as i:
                for j in (2, 3):
                    load_fw(i * 2 + j, i * 2 + j, j % 2)
            load_fw(FC - 1, FC - 1, (FC - 1) % 2)
            for f in range(3):
                load_fw(FC + f, f, (FC + f) % 2)
            store(0)
            with sp.Fori(0, (FC - 3) // 2) as i:
                for j in (3, 4):
                    load_fw(i * 2 + (FC + j), i * 2 + j, (FC + j) % 2)
            store(1)
            sp.wait_ge(out_stored, 16 * B)

        @block.tensor
        def _(pe):
            def product(out_ps, lhs, rhs, first=True, last=True):
                (lh, ll), (rh, rl) = lhs, rhs
                pe.matmul(out_ps, lh, rh, start=first, stop=False)
                pe.matmul(out_ps, lh, rl, start=False, stop=False)
                return pe.matmul(out_ps, ll, rh, start=False, stop=last)

            def transpose_xn(b, total):
                pe.wait_ge(ln_rows, total + 1)
                if total < B:
                    if total > 1:
                        pe.wait_ge(xn_lo_ok, total - 1)
                else:
                    if b % 2 == 0 and b > 0:
                        pe.wait_ge(v_lo_ok, UNITS)
                    else:
                        pe.wait_ge(k_rot_ok, UNITS - B + min(b + 6, B))
                    pe.wait_ge(xn_lo_ok, total)
                for k in range(KC):
                    mm = pe.transpose(ps_x[total // B][b][:, k * P:(k + 1) * P], xn[:, b % 2, k * P:(k + 1) * P], idn[:, :])
                mm.then_inc(xt_done, 1)

            def project_q(n, head, half, ps, parts, rows=slice(0, ROWS)):
                for k in parts:
                    mm = product(ps[:, rows], (wq_hi[:, head, k, :], wq_lo[:, head, k, :]),
                                 (xn_hi[:, half, k, rows], xn_lo[:, half, k, rows]), k == 0, k == KC - 1)
                if KC - 1 in parts and rows.stop == ROWS:
                    mm.then_inc(q_done, 1)

            def project_kv(b, ps=ps_kv):
                for k in range(KC):
                    c = slice((b * KC + k) * P, (b * KC + k + 1) * P)
                    mm = product(ps, (c_hi[:, c], c_lo[:, c]), (wkv_hi[:, k, :], wkv_lo[:, k, :]),
                                 k == 0, k == KC - 1)
                mm.then_inc(kv_done, 1)

            def scores(b):
                for h in range(HPG):
                    q = q_rot[:, b // HALF, h, (b % HALF) * P:(b % HALF + 1) * P]
                    mm = pe.matmul(ps_s[:, h * P:(h + 1) * P], q, k_rot[:, b, :], start=True, stop=True)
                mm.then_inc(s_done, 1)

            def transpose_k(n, first=False):
                pe.wait_ge(k_rows_ok, n + 1)
                if not first:
                    pe.wait_ge(k_rot_ok, n)
                pe.transpose(ps_kt, k_rows[:, :], idn[:, :]).then_inc(kt_done, 1)

            def first_q(n, half, rows=slice(0, ROWS)):
                if n < HPG:
                    pe.wait_ge(wq_hi_ok, n + 1)
                    pe.wait_ge(wq_lo_ok, n + 1)
                if n >= 2:
                    pe.wait_ge(q_cos_ok, n - 1)
                project_q(n, n % HPG, half, ps_q[n % 2], range(KC), rows)

            def first_kv(n):
                pe.wait_ge(c_hi_ok, n + 1)
                pe.wait_ge(c_lo_ok, n + 1)
                if n == 0:
                    pe.wait_ge(wkv_hi_ok, 1)
                    pe.wait_ge(wkv_lo_ok, 1)
                elif n == 1:
                    pe.wait_ge(v_lo_ok, 1)
                elif n == 3:
                    pe.wait_ge(v_lo_ok, 2)
                project_kv(n, ps_kv2 if n == 2 else ps_kv)

            def keep_clock(products):
                for _ in range(products):
                    pe.matmul(ps_s[:, 0:P], idn[:, :], idn[:, :], start=True, stop=True)

            pe.wait_ge(ident_in, 16)
            keep_clock(WARM[0])
            for b in range(HALF):
                transpose_xn(b, b)
                if b < 2:
                    keep_clock(WARM[b + 1])
            for upto in (HALF // 2, HALF):
                pe.wait_ge(xn_hi_ok, upto)
                pe.wait_ge(xn_lo_ok, upto)
                for n in range(2):
                    first_q(n, 0, slice((upto - HALF // 2) * P, upto * P))
            first_kv(0)
            first_q(2, 0)
            transpose_k(0, first=True)
            transpose_xn(HALF, HALF)
            transpose_xn(HALF + 1, HALF + 1)
            first_q(3, 0)
            first_kv(1)
            first_kv(2)
            transpose_xn(HALF + 2, HALF + 2)
            transpose_xn(HALF + 3, HALF + 3)
            pe.wait_ge(q_rot_ok, HPG)
            pe.wait_ge(k_rot_ok, 1)
            scores(0)
            transpose_k(1)
            first_kv(3)
            pe.wait_ge(xn_hi_ok, B)
            pe.wait_ge(xn_lo_ok, B)
            first_q(HPG, 1)
            transpose_k(2)
            pe.wait_ge(c_hi_ok, B)
            pe.wait_ge(c_lo_dve_ok, 2)

            def project_out(g, b):
                n = g * B + (b + 1)
                pe.wait_ge(ot_hi_ok, n)
                pe.wait_ge(ot_lo_ok, n)
                for h in range(HPG):
                    if b == 0:
                        pe.wait_ge(wo_hi_ok, g * HPG + (h + 1))
                        pe.wait_ge(wo_lo_ok, g * HPG + (h + 1))
                    c = slice(h * P, (h + 1) * P)
                    mm = product(ps_wo[:, :], (ot_hi[:, c], ot_lo[:, c]), (wo_hi[:, h, :], wo_lo[:, h, :]),
                                 h == 0, h == HPG - 1)
                mm.then_inc(wo_done, 1)

            def gate_or_up(which, ps, done, t, half, par):
                pe.wait_ge(gu_hi_ok, t + 1)
                pe.wait_ge(gu_lo_ok, t + 1)
                for k in range(KC):
                    c = slice((which * KC + k) * P, (which * KC + k + 1) * P)
                    mm = product(ps[:, :], (fw_hi[par][:, c], fw_lo[par][:, c]),
                                 (xn_hi[:, half, k, :], xn_lo[:, half, k, :]), k == 0, k == KC - 1)
                mm.then_inc(done, 1)

            def gate(t, half, par):
                gate_or_up(0, ps_gate[par], gate_done, t, half, par)

            def up(t, half, par):
                gate_or_up(1, ps_up[par], up_done, t, half, par)

            def spread_probs(n, b):
                pe.wait_ge(prob_ok, n)
                for h in range(HPG):
                    mm = pe.transpose(ps_pt[:, h * P:(h + 1) * P], prob[:, b % 2, h, :], idn[:, :])
                mm.then_inc(pt_done, 1)

            def weigh_values(n, b):
                pe.wait_ge(pt_hi_ok, n)
                pe.wait_ge(pt_lo_ok, n)
                pe.wait_ge(v_hi_ok, n)
                pe.wait_ge(v_lo_ok, n)
                product(ps_o[:, :], (v_hi[:, b, :], v_lo[:, b, :]), (pt_hi[:, :], pt_lo[:, :])).then_inc(o_done, 1)

            def slot(g, b, last):
                u = g * B
                spread_probs(u + (b + 1), b)
                pe.wait_ge(q_rot_ok, u + (4 * ((b + 1) // 4) + 4))
                pe.wait_ge(k_rot_ok, u + (b + 2))
                scores((b + 1) % B)
                n = b + LEAD_Q
                if n >= B:
                    pe.wait_ge(wq_hi_ok, g * HPG + (HPG + min(n - B, HPG - 1) + 1))
                    pe.wait_ge(wq_lo_ok, g * HPG + (HPG + min(n - B, HPG - 1) + 1))
                pe.wait_ge(q_cos_ok, u + (n - 1))
                where = (n, n % HPG, (n // HPG) % 2, ps_q[n % 2])
                project_q(*where, range(0, KC // 2))
                weigh_values(u + (b + 1), b)
                project_q(*where, range(KC // 2, KC))
                transpose_k(u + (b + 3))
                n = b + LEAD_KV
                if n >= B:
                    pe.wait_ge(wkv_hi_ok, g + 2)
                    pe.wait_ge(wkv_lo_ok, g + 2)
                elif n >= HALF + 2 and not last:
                    pe.wait_ge(c_lo_ok, n - 1)
                pe.wait_ge(v_lo_ok, u + n)
                project_kv(n % B)
                project_out(g, b)
                if last and b == 1:
                    scores_ahead(b + 2)

            U = UNITS - B

            def scores_ahead(b):
                if b == HALF:
                    pe.wait_ge(q_rot_ok, UNITS)
                pe.wait_ge(k_rot_ok, U + b + 1)
                pe.wait_ge(exp_ok, U + b)
                scores(b)

            def closing(b):
                spread_probs(U + b + 1, b)
                if b == 2:
                    pe.wait_ge(q_cos_ok, UNITS - 2)
                    project_q(B - 1, HPG - 1, 1, ps_q[1], range(0, KC - 1))
                    weigh_values(U + b + 1, b)
                    project_q(B - 1, HPG - 1, 1, ps_q[1], range(KC - 1, KC))
                    transpose_k(U + 5)
                    pe.wait_ge(v_lo_ok, U + 6)
                    project_kv(6)
                    project_out(G - 1, b)
                    transpose_xn(0, B)
                    scores_ahead(b + 2)
                elif b == 3:
                    pe.wait_ge(xn_lo_ok, B + 1)
                    transpose_k(U + 6)
                    pe.wait_ge(v_lo_ok, U + 7)
                    project_kv(7)
                    weigh_values(U + b + 1, b)
                    scores_ahead(b + 2)
                    transpose_xn(1, B + 1)
                else:
                    pe.wait_ge(acc_ok, U + b - 1)
                    project_out(G - 1, b - 1)
                    weigh_values(U + b + 1, b)
                    if b == HALF:
                        pe.wait_ge(xn_lo_ok, B + 2)
                        transpose_k(U + 7)
                    if b + 2 < B:
                        scores_ahead(b + 2)
                    elif b == B - 2:
                        pe.wait_ge(xn_hi_ok, B + HALF)
                        pe.wait_ge(xn_lo_ok, B + HALF)
                        gate(0, 0, 0)
                    else:
                        up(0, 0, 0)
                    transpose_xn(b - 2, B + b - 2)

            attention_slots(pe, slot, closing)
            pe.wait_ge(acc_ok, UNITS - 1)
            project_out(G - 1, B - 1)
            transpose_xn(B - 2, 2 * B - 2)

            def step(i, half, j):
                t0 = half * FC + j
                t, par = i * 2 + t0, t0 % 2
                first, last = j == 0, j == FC - 1
                if not (half == 1 and last):
                    if last:
                        pe.wait_ge(xn_hi_ok, 2 * B)
                        pe.wait_ge(xn_lo_ok, 2 * B)
                    if t0 > 0:
                        pe.wait_ge(silu_ok, t)
                        pe.wait_ge(hid_ok, t)
                    gate(t + 1, 1 if last else half, 1 - par)
                    up(t + 1, 1 if last else half, 1 - par)
                    if t0 == 0:
                        transpose_xn(B - 1, 2 * B - 1)
                pe.wait_ge(hid_hi_ok, t + 1)
                pe.wait_ge(hid_lo_ok, t + 1)
                pe.wait_ge(dn_hi_ok, t + 1)
                pe.wait_ge(dn_lo_ok, t + 1)
                if t0 == 0:
                    pe.wait_ge(xn_lo_ok, 2 * B - 1)
                elif first:
                    pe.wait_ge(y_ok, HALF)
                for r in range(HALF):
                    c = slice(r * P, (r + 1) * P)
                    if t0 == 0 and r == HALF - 1:
                        pe.wait_ge(xn_lo_ok, 2 * B)
                    mm = product(ps_y[r][:, :], (hid_hi[par][:, c], hid_lo[par][:, c]),
                                 (fw_hi[par][:, GU:FW], fw_lo[par][:, GU:FW]), first, last)
                    if last:
                        mm.then_inc(y_done, 1)

            mlp_steps(pe, step)

        @block.scalar
        def _(act):
            def split_c(b):
                act.wait_ge(c_in[b], 16)
                act.activation(c_part(c_hi, b), q_rot[:, b // HALF, b % HALF, :], ACT.Copy).then_inc(c_hi_ok, 1)

            def split_wq(h, loaded, by=wq_in):
                act.wait_ge(by, loaded)
                act.activation(wq_hi[:, h, :, :].rearrange("p k r -> p (k r)"),
                               wq_raw[:, h * KC * P:(h + 1) * KC * P], ACT.Copy).then_inc(wq_hi_ok, 1)

            def split_wkv(g16):
                act.wait_ge(wkv_in, g16)
                act.activation(wkv_hi[:, :, :].rearrange("p k r -> p (k r)"), wkv_raw[:, :], ACT.Copy).then_inc(wkv_hi_ok, 1)

            def split_xn(b, total):
                act.wait_ge(xt_done, total + 1)
                act.activation(xn_part(xn_hi, b), chunks(ps_x[total // B][b][:, :]), ACT.Copy).then_inc(xn_hi_ok, 1)

            def swap_q(ps, nq):
                act.wait_ge(q_done, nq + 1)
                act.wait_ge(q_sin_ok, nq)
                act.activation(q_swap[0:P // 2, :], ps[P // 2:P, :], ACT.Copy)
                act.activation(q_swap[P // 2:P, :], ps[0:P // 2, :], ACT.Copy).then_inc(q_swap_ok, 1)

            def take_v(b, n, ps=ps_kv):
                act.wait_ge(kv_done, n + 1)
                act.activation(v_hi[:, b, :], ps[:, P:2 * P], ACT.Copy).then_inc(v_hi_ok, 1)

            def take_kt(b, n):
                act.wait_ge(kt_done, n + 1)
                act.activation(k_rot[:, b, :], ps_kt, ACT.Copy).then_inc(k_rot_ok, 1)

            def exponentials(par, n):
                act.wait_ge(s_max_ok, n + 1)
                for h in range(HPG):
                    e = act.activation(prob[:, par, h, :], ps_s[:, h * P:(h + 1) * P], ACT.Exp,
                                       bias=nmax[:, par, h:h + 1], scale=-1.0, accum_out=rsum[:, par, h:h + 1])
                e.then_inc(exp_ok, 1)

            split_wq(0, 16, wq_first_in)
            split_xn(0, 0)
            split_xn(1, 1)
            split_wq(1, 16)
            split_xn(2, 2)
            split_xn(3, 3)
            split_wkv(16)
            split_c(0)
            split_wq(2, 16)
            split_wq(3, 16)
            split_c(1)
            swap_q(ps_q[0], 0)
            take_v(0, 0)
            split_c(2)
            split_c(3)
            swap_q(ps_q[1], 1)
            split_c(4)
            split_c(5)
            swap_q(ps_q[0], 2)
            take_kt(0, 0)
            split_xn(HALF, HALF)
            split_xn(HALF + 1, HALF + 1)
            act.wait_ge(bound_cmp, 1)
            act.activation(bound[:, :, :], bound[:, :, :], ACT.Copy, scale=-NO_BOUND, bias=-MASKED).then_inc(bound_ok, 1)
            swap_q(ps_q[1], 3)
            take_v(1, 1)
            split_c(6)
            take_v(2, 2, ps_kv2)
            split_xn(HALF + 2, HALF + 2)
            split_xn(HALF + 3, HALF + 3)
            split_c(7)
            take_kt(1, 1)
            act.wait_ge(gates_in, 16)
            act.activation(gate_tanh[:, :], gate_in[:, :], ACT.Tanh).then_inc(tanh_ok, 1)
            exponentials(0, 0)
            take_v(3, 3)
            swap_q(ps_q[0], HPG)
            take_kt(2, 2)

            def split_gu(par, loaded):
                act.wait_ge(gu_in[par], loaded)
                act.activation(fw_hi[par][:, 0:GU], fw_raw[par][:, 0:GU], ACT.Copy).then_inc(gu_hi_ok, 1)

            def ln_centre(b):
                act.wait_ge(ln_mean, b + 1)
                act.wait_ge(xt_done, B + b - 1)
                act.activation(xn[:, b % 2, :], acc[:, b, :], ACT.Identity,
                               bias=minus_mean[:, b:b + 1]).then_inc(ln_centred, 1)

            def ln_scale(b):
                act.wait_ge(ln_centred, b + 1)
                act.wait_ge(ln_rstd, HALF + b + 1)
                act.activation(xn[:, b % 2, :], xn[:, b % 2, :], ACT.Copy,
                               scale=rstd[:, b:b + 1]).then_inc(ln_rows, 1)

            def take_probs(n):
                act.wait_ge(pt_done, n)
                act.activation(pt_hi[:, :], ps_pt[:, :], ACT.Copy).then_inc(pt_hi_ok, 1)

            def take_outputs(n):
                act.wait_ge(o_done, n)
                act.activation(ot_hi[:, :], ps_o[:, :], ACT.Copy).then_inc(ot_hi_ok, 1)

            def slot(g, b, last):
                u = g * B
                take_probs(u + (b + 1))
                if b == 0:
                    act.wait_ge(wo_in, g * 16 + 16)
                    for h in range(HPG):
                        act.activation(wo_hi[:, h, :], wo_raw[:, h * DM:(h + 1) * DM], ACT.Copy).then_inc(wo_hi_ok, 1)
                take_outputs(u + (b + 1))
                exponentials((b + 1) % 2, u + (b + 1))
                n = b + LEAD_Q
                swap_q(ps_q[n % 2], u + n)
                take_kt((b + 3) % B, u + (b + 3))
                n = b + LEAD_KV
                take_v(n % B, u + n)
                if last:
                    if b == 1:
                        split_gu(0, 16)
                        ln_centre(0)
                    return
                if 1 <= b <= HPG:
                    split_wq(b - 1, g * 16 + 32)
                if b == HALF - 1:
                    split_wkv(g * 16 + 32)

            def closing(b):
                U = UNITS - B
                take_probs(U + b + 1)
                if b == 2:
                    take_outputs(U + b + 1)
                    swap_q(ps_q[1], UNITS - 1)
                    take_kt(5, U + 5)
                    take_v(6, U + 6)
                    ln_scale(0)
                    exponentials(1, U + 3)
                    split_xn(0, B)
                    split_gu(1, 16)
                else:
                    if b == 3:
                        take_kt(6, U + 6)
                    if b + 1 < B:
                        exponentials((b + 1) % 2, U + b + 1)
                    ln_scale(b - 2)
                    if b == 3:
                        take_v(7, U + 7)
                    take_outputs(U + b + 1)
                    if b == HALF:
                        take_kt(7, U + 7)
                    split_xn(b - 2, B + b - 2)
                ln_centre(b - 1)

            attention_slots(act, slot, closing)
            ln_scale(B - 2)
            split_xn(B - 2, 2 * B - 2)

            def step(i, half, j):
                t0 = half * FC + j
                t, par = i * 2 + t0, t0 % 2
                act.wait_ge(gate_done, t + 1)
                act.activation(silu[par][:, :], ps_gate[par][:, :], ACT.Silu).then_inc(silu_ok, 1)
                act.wait_ge(dn_in[par], fw_loads(i, t0))
                act.activation(fw_hi[par][:, GU:FW], fw_raw[par][:, GU:FW], ACT.Copy).then_inc(dn_hi_ok, 1)
                if t0 == 0:
                    act.wait_ge(up_done, 1)
                    split_gu(0, fw_loads(0, 2))
                    ln_centre(B - 1)
                act.wait_ge(hid_ok, t + 1)
                act.activation(hid_hi[par][:, :], hid[par], ACT.Copy).then_inc(hid_hi_ok, 1)
                if t0 == 0:
                    ln_scale(B - 1)
                    split_xn(B - 1, 2 * B - 1)
                elif t0 < 2 * FC - 2:
                    split_gu(par, fw_loads(i, t0 + 2))

            mlp_steps(act, step)

        @block.vector
        def _(dve):
            def sub(out_lo, whole, hi):
                return dve.tensor_tensor(out_lo, whole, f32(hi), ALU.subtract)

            def ln_moments(b, total):
                dve.wait_ge(ln_stats, total + 1)
                dve.bn_aggr(meanvar[:, b, :], stats[:, b, :]).then_inc(ln_aggr, 1)

            def ln_add_eps(b, total):
                dve.wait_ge(ln_aggr, total + 1)
                dve.tensor_scalar(vareps[:, b:b + 1], meanvar[:, b, 1:2], LN_EPS, None, ALU.add).then_inc(ln_var, 1)

            def ln_row(b, total):
                if total < HALF:
                    dve.wait_ge(ln_rstd, total + 1)
                else:
                    dve.wait_ge(ln_rstd4, 1)
                if total > 1:
                    dve.wait_ge(xt_done, total - 1)
                dve.tensor_scalar(xn[:, b % 2, :], acc[:, b, :], meanvar[:, b, 0:1], rstd[:, b:b + 1],
                                  ALU.subtract, ALU.mult).then_inc(ln_rows, 1)

            def split_xn(b, total):
                dve.wait_ge(xn_hi_ok, total + 1)
                sub(xn_part(xn_lo, b), chunks(ps_x[total // B][b][:, :]), xn_part(xn_hi, b)).then_inc(xn_lo_ok, 1)

            def rope_k(n, ps=ps_kv):
                dve.wait_ge(v_hi_ok, n + 1)
                dve.tensor_tensor(k_c[:, :], ps[:, 0:P], cos_k, ALU.mult).then_inc(k_cos_ok, 1)
                lo, up = slice(0, P // 2), slice(P // 2, P)
                dve.tensor_tensor(k_s[:, lo], ps[:, up], sin_k[:, lo], ALU.mult)
                dve.tensor_tensor(k_s[:, up], ps[:, lo], sin_k[:, up], ALU.mult).then_inc(k_sin_ok, 1)
                dve.wait_ge(k_cos_ok, n + 1)
                dve.wait_ge(k_sin_ok, n + 1)
                dve.wait_ge(kt_done, n)
                dve.tensor_tensor(k_rows[:, :], k_c[:, :], k_s[:, :], ALU.add).then_inc(k_rows_ok, 1)

            def split_v(b, n, ps=ps_kv):
                sub(v_lo[:, b, :], ps[:, P:2 * P], v_hi[:, b, :]).then_inc(v_lo_ok, 1)

            def split_wkv(count):
                dve.wait_ge(wkv_hi_ok, count)
                sub(wkv_lo[:, :, :].rearrange("p k r -> p (k r)"), wkv_raw[:, :],
                    wkv_hi[:, :, :].rearrange("p k r -> p (k r)")).then_inc(wkv_lo_ok, 1)

            def rope_q(ps, n):
                dve.wait_ge(q_swap_ok, n + 1)
                dve.wait_ge(q_rot_ok, n)
                dve.tensor_tensor(heads(q_c[:, :]), heads(ps[:, :]), over_heads(cos_q), ALU.mult).then_inc(q_cos_ok, 1)
                dve.tensor_tensor(heads(q_s[:, :]), heads(q_swap[:, :]), over_heads(sin_q), ALU.mult).then_inc(q_sin_ok, 1)

            def row_max(b, par, n):
                dve.wait_ge(s_done, n + 1)
                dve.tensor_tensor(heads(ps_s[:, :]), heads(ps_s[:, :]), over_heads(bound[:, b, :]),
                                  ALU.max).then_inc(s_bound_ok, 1)
                dve.wait_ge(s_bound_ok, n + 1)
                dve.tensor_reduce(nmax[:, par, :], heads(ps_s[:, :]), AX_X, ALU.min).then_inc(s_max_ok, 1)

            def invert_sums(par, n):
                dve.wait_ge(exp_ok, n + 1)
                dve.reciprocal(rinv[:, par, :], rsum[:, par, :]).then_inc(rinv_ok, 1)

            def split_c(b):
                dve.wait_ge(c_hi_ok, b + 1)
                sub(c_part(c_lo, b), q_rot[:, b // HALF, b % HALF, :], c_part(c_hi, b)).then_inc(c_lo_dve_ok, 1)

            def ln_first(b):
                dve.wait_ge(x_in[b], 16)
                dve.bn_stats(stats[:, b, :], acc[:, b, :]).then_inc(ln_stats, 1)

            def rope_kv(n, ps=ps_kv):
                if n > 0:
                    dve.wait_ge(k_rows_ok, n)
                rope_k(n, ps)
                split_v(n, n, ps)

            ln_first(0)
            ln_first(1)
            ln_moments(0, 0)
            ln_first(2)
            ln_add_eps(0, 0)
            ln_moments(1, 1)
            ln_row(0, 0)
            ln_add_eps(1, 1)
            ln_moments(2, 2)
            ln_first(3)
            ln_add_eps(2, 2)
            ln_row(1, 1)
            ln_moments(3, 3)
            ln_add_eps(3, 3)
            split_xn(0, 0)
            ln_row(2, 2)
            ln_row(3, 3)
            split_xn(1, 1)
            split_xn(2, 2)
            split_xn(3, 3)
            split_wkv(1)
            for b in range(HALF, B):
                ln_first(b)
            for b in range(HALF, B):
                ln_moments(b, b)
            dve.wait_ge(ln_aggr, B)
            dve.tensor_scalar(vareps[:, HALF:B], meanvar[:, HALF:B, 1], LN_EPS, None, ALU.add).then_inc(ln_var4, 1)
            dve.wait_ge(tables_in, 16)
            rope_q(ps_q[0], 0)
            rope_kv(0)
            ln_row(HALF, HALF)
            ln_row(HALF + 1, HALF + 1)
            rope_q(ps_q[1], 1)
            dve.wait_ge(mask_in, 16)
            dve.tensor_scalar(bound[:, :, :], bound[:, :, :], 0.0, None, ALU.not_equal).then_inc(bound_cmp, 1)
            ln_row(HALF + 2, HALF + 2)
            ln_row(HALF + 3, HALF + 3)
            rope_q(ps_q[0], 2)
            split_xn(HALF, HALF)
            split_xn(HALF + 1, HALF + 1)
            rope_q(ps_q[1], 3)
            rope_kv(1)
            split_xn(HALF + 2, HALF + 2)
            split_xn(HALF + 3, HALF + 3)
            dve.wait_ge(bound_ok, 1)
            row_max(0, 0, 0)
            rope_kv(2, ps_kv2)
            split_c(HALF)
            invert_sums(0, 0)
            split_c(HALF + 1)
            rope_kv(3)
            rope_q(ps_q[0], HPG)
            dve.wait_ge(tanh_ok, 1)

            def ln_stats_second(b):
                dve.wait_ge(acc_ok, UNITS - B + b + 1)
                dve.bn_stats(stats[:, b, :], acc[:, b, :]).then_inc(ln_stats, 1)

            def ln_moments_second(b):
                ln_moments(b, B + b)
                ln_add_eps(b, B + b)
                dve.tensor_scalar(minus_mean[:, b:b + 1], meanvar[:, b, 0:1], -1.0, None, ALU.mult).then_inc(ln_mean, 1)

            def add_out(b, n):
                dve.wait_ge(wo_done, n + 1)
                dve.scalar_tensor_tensor(out=acc[:, b, :], in0=ps_wo[:, :], scalar=gate_tanh[:, 0:1],
                                         in1=acc[:, b, :], op0=ALU.mult, op1=ALU.add).then_inc(acc_ok, 1)

            def split_probs(n):
                dve.wait_ge(pt_hi_ok, n)
                sub(pt_lo[:, :], ps_pt[:, :], pt_hi[:, :]).then_inc(pt_lo_ok, 1)

            def split_outputs(n):
                dve.wait_ge(ot_hi_ok, n)
                sub(ot_lo[:, :], ps_o[:, :], ot_hi[:, :]).then_inc(ot_lo_ok, 1)

            def slot(g, b, last):
                u = g * B
                split_probs(u + (b + 1))
                row_max((b + 1) % B, (b + 1) % 2, u + (b + 1))
                split_outputs(u + (b + 1))
                invert_sums((b + 1) % 2, u + (b + 1))
                n = b + LEAD_Q
                rope_q(ps_q[n % 2], u + n)
                n = b + LEAD_KV
                rope_k(u + n)
                split_v(n % B, u + n)
                if not last and b == HALF - 1:
                    split_wkv(g + 2)
                if last and b == 1:
                    ln_stats_second(0)
                    ln_moments_second(0)
                add_out(b, u + b)

            def closing(b):
                U = UNITS - B
                if b == 2:
                    split_probs(U + 3)
                    row_max(3, 1, U + 3)
                    split_outputs(U + 3)
                    ln_stats_second(1)
                    ln_moments_second(1)
                    rope_q(ps_q[1], UNITS - 1)
                    rope_k(U + 6)
                    split_v(6, U + 6)
                    invert_sums(1, U + 3)
                    split_xn(0, B)
                elif b == 3:
                    row_max(4, 0, U + 4)
                    split_probs(U + 4)
                    add_out(2, U + 2)
                    ln_stats_second(2)
                    ln_moments_second(2)
                    invert_sums(0, U + 4)
                    rope_k(U + 7)
                    split_v(7, U + 7)
                    split_outputs(U + 4)
                else:
                    if b + 1 < B:
                        row_max(b + 1, (b + 1) % 2, U + b + 1)
                    split_probs(U + b + 1)
                    split_xn(b - 3, B + b - 3)
                    if b + 1 < B:
                        invert_sums((b + 1) % 2, U + b + 1)
                    add_out(b - 1, U + b - 1)
                    ln_stats_second(b - 1)
                    split_outputs(U + b + 1)
                    ln_moments_second(b - 1)

            attention_slots(dve, slot, closing)
            split_xn(B - 3, 2 * B - 3)
            split_xn(B - 2, 2 * B - 2)
            add_out(B - 1, UNITS - 1)
            ln_stats_second(B - 1)
            ln_moments_second(B - 1)

            def step(i, half, j):
                t0 = half * FC + j
                t, par = i * 2 + t0, t0 % 2
                dve.wait_ge(silu_ok, t + 1)
                dve.wait_ge(up_done, t + 1)
                dve.tensor_tensor(hid[par], ps_up[par][:, :], silu[par][:, :], ALU.mult).then_inc(hid_ok, 1)
                dve.wait_ge(hid_hi_ok, t + 1)
                sub(hid_lo[par][:, :], hid[par], hid_hi[par][:, :]).then_inc(hid_lo_ok, 1)
                if t0 == 0:
                    split_xn(B - 1, 2 * B - 1)
                if j == FC - 1:
                    for r in range(HALF):
                        b = half * HALF + r
                        dve.wait_ge(y_done, b + 1)
                        dve.scalar_tensor_tensor(out=acc[:, b, :], in0=ps_y[r][:, :], scalar=gate_tanh[:, 1:2],
                                                 in1=acc[:, b, :], op0=ALU.mult, op1=ALU.add).then_inc(y_ok, 1)

            mlp_steps(dve, step)

        @block.gpsimd
        def _(pool):
            def sub(out_lo, whole, hi):
                return pool.tensor_tensor(out_lo, whole, f32(hi), ALU.subtract)

            def split_c(b):
                pool.wait_ge(c_hi_ok, b + 1)
                sub(c_part(c_lo, b), q_rot[:, b // HALF, b % HALF, :], c_part(c_hi, b)).then_inc(c_lo_ok, 1)

            def ln_power(b, count):
                pool.wait_ge(ln_var, count)
                pool.tensor_tensor(rstd[:, b:b + 1], vareps[:, b:b + 1], minus_half[:, b:b + 1],
                                   ALU.pow).then_inc(ln_rstd, 1)

            def split_wq(h, count):
                pool.wait_ge(wq_hi_ok, count)
                sub(wq_lo[:, h, :, :].rearrange("p k r -> p (k r)"), wq_raw[:, h * KC * P:(h + 1) * KC * P],
                    wq_hi[:, h, :, :].rearrange("p k r -> p (k r)")).then_inc(wq_lo_ok, 1)

            def add_q(half, head, n):
                pool.wait_ge(q_cos_ok, n + 1)
                pool.wait_ge(q_sin_ok, n + 1)
                pool.tensor_tensor(q_rot[:, half, head, :], q_c[:, :], q_s[:, :], ALU.add).then_inc(q_rot_ok, 1)

            def normalise(par, n):
                pool.wait_ge(rinv_ok, n + 1)
                p4 = prob[:, par, :, :]
                pool.tensor_tensor(p4, p4, rinv[:, par, :].unsqueeze(2).broadcast_to([P, HPG, P]),
                                   ALU.mult).then_inc(prob_ok, 1)

            pool.memset(minus_half[:, :], -0.5).then_inc(half_ok, 1)
            pool.wait_ge(half_ok, 1)
            for b in range(HALF):
                ln_power(b, b + 1)
            split_wq(0, 1)
            split_wq(1, 2)
            split_c(0)
            split_wq(2, 3)
            split_wq(3, 4)
            pool.wait_ge(ln_var4, 1)
            pool.tensor_tensor(rstd[:, HALF:B], vareps[:, HALF:B], minus_half[:, HALF:B], ALU.pow).then_inc(ln_rstd4, 1)
            for n in range(HPG):
                pool.wait_ge(c_lo_ok, n + 1)
                add_q(0, n, n)
                if n + 1 < HALF:
                    split_c(n + 1)
            split_c(B - 2)
            normalise(0, 0)
            split_c(B - 1)
            pool.wait_ge(c_lo_ok, B - 2)
            pool.wait_ge(c_lo_dve_ok, 2)
            add_q(1, 0, HPG)

            def split_gu(t, par):
                pool.wait_ge(gu_hi_ok, t + 1)
                sub(fw_lo[par][:, 0:GU], fw_raw[par][:, 0:GU], fw_hi[par][:, 0:GU]).then_inc(gu_lo_ok, 1)

            def slot(g, b, last):
                u = g * B
                if b == 0:
                    for h in range(HPG):
                        pool.wait_ge(wo_hi_ok, g * HPG + (h + 1))
                        sub(wo_lo[:, h, :], wo_raw[:, h * DM:(h + 1) * DM], wo_hi[:, h, :]).then_inc(wo_lo_ok, 1)
                normalise((b + 1) % 2, u + (b + 1))
                n = b + LEAD_Q
                add_q((n // HPG) % 2, n % HPG, u + n)
                if last:
                    if b == 1:
                        split_gu(0, 0)
                        ln_power(0, HALF + 1)
                elif 1 <= b <= HPG:
                    split_wq(b - 1, g * HPG + (HPG + b))

            def closing(b):
                if b == 3:
                    split_gu(1, 1)
                if b == 2:
                    add_q(1, HPG - 1, UNITS - 1)
                if b + 1 < B:
                    normalise((b + 1) % 2, UNITS - B + b + 1)
                ln_power(b - 1, HALF + b)

            attention_slots(pool, slot, closing)
            ln_power(B - 1, HALF + B)

            def step(i, half, j):
                t0 = half * FC + j
                t, par = i * 2 + t0, t0 % 2
                pool.wait_ge(dn_hi_ok, t + 1)
                sub(fw_lo[par][:, GU:FW], fw_raw[par][:, GU:FW], fw_hi[par][:, GU:FW]).then_inc(dn_lo_ok, 1)
                if t0 < 2 * FC - 2:
                    split_gu(t + 2, par)

            mlp_steps(pool, step)


def rope_tables(n_rows, dim, np):
    inv_freq = 1.0 / np.float32(10000.0) ** (np.arange(0, dim, 2, dtype=np.float32) / np.float32(dim))
    ang = np.arange(n_rows, dtype=np.float32)[:, None] * inv_freq[None, :].astype(np.float32)
    cos, sin = np.cos(ang), np.sin(ang)
    cos = np.concatenate([cos, cos], axis=1)
    sin = np.concatenate([-sin, sin], axis=1)
    by = -1.0 / np.sqrt(np.float64(dim))
    return np.stack([cos.T * by, sin.T * by, cos, sin]).astype(np.float32)


def kernel(x, ctx_4096, mask_BxSxS2_ff1, g_xattn, g_ffn, L0_xattn_wq, L0_xattn_wk, L0_xattn_wv, L0_xattn_wo,
           L0_ffn_W_gate, L0_ffn_W_up, L0_ffn_W_down):
    import numpy as np
    import concourse.bacc as bacc
    from concourse.bass_utils import run_bass_kernel_spmd

    x, c, mask, g_x, g_f, wq, wk, wv, wo, w_gate, w_up, w_down = (
        np.asarray(a) for a in (x, ctx_4096, mask_BxSxS2_ff1, g_xattn, g_ffn, L0_xattn_wq, L0_xattn_wk,
                                L0_xattn_wv, L0_xattn_wo, L0_ffn_W_gate, L0_ffn_W_up, L0_ffn_W_down))
    B, S, DM = x.shape
    KC, G = DM // P, wk.shape[1] // P
    HPG = wq.shape[1] // (G * P)
    F = w_gate.shape[0]
    FC = -(-F // P)
    pad = FC * P - F

    def kcols(w, heads):
        return w.reshape(KC, P, G, heads, P).transpose(2, 1, 3, 0, 4)

    def chunked(w):
        return np.pad(w, ((0, pad), (0, 0))).reshape(FC, P, KC, P).transpose(0, 3, 2, 1)

    wkv = np.concatenate([kcols(wk, 1)[:, :, 0], kcols(wv, 1)[:, :, 0]], axis=3)
    down = np.pad(w_down.T, ((0, pad), (0, 0))).reshape(FC, P, DM)
    w_ffn = np.concatenate([chunked(w_gate).reshape(FC, P, KC * P), chunked(w_up).reshape(FC, P, KC * P), down], axis=2)
    gates = np.empty((P, 2), x.dtype)
    gates[:, 0], gates[:, 1] = g_x[0], g_f[0]
    arrays = {
        "x": x,
        "ctx_t": c.reshape(B, S, KC, P).transpose(0, 3, 2, 1),
        "mask": mask.transpose(1, 0, 2),
        "gates": gates,
        "wq": kcols(wq, HPG).reshape(G, P, HPG * KC * P),
        "wkv": wkv.reshape(G, P, KC * 2 * P),
        "wo": wo.reshape(G, HPG, P, DM).transpose(0, 2, 1, 3).reshape(G, P, HPG * DM),
        "w_ffn": w_ffn,
        "rope": rope_tables(S, P, np),
        "ident": np.eye(P, dtype=np.float32),
    }
    arrays = {f"in_{n}": np.ascontiguousarray(a) for n, a in arrays.items()}
    nc = bacc.Bacc("TRN2", target_bir_lowering=False, num_devices=1)
    ins = [nc.dram_tensor(n, a.shape, mybir.dt.from_np(a.dtype), kind="ExternalInput").ap() for n, a in arrays.items()]
    out = nc.dram_tensor("out_0", (B, S, DM), F32, kind="ExternalOutput").ap()
    gated_cross_attention_block(nc, *ins, out)
    r = run_bass_kernel_spmd(nc, [arrays], core_ids=[0])
    return r.results[0]["out_0"]
```
